# Optimizing a Trainium2 kernel written in Bass

```python
import numpy as np
import jax
import jax.numpy as jnp

def _softmax(x, axis=-1):
    return jax.nn.softmax(x, axis=axis)

def _gelu(x):
    return jax.nn.gelu(x, approximate=True)

def _silu(x):
    return jax.nn.silu(x)

def _sigmoid(x):
    return jax.nn.sigmoid(x)

def _layernorm(x, axis=-1, eps=1e-05):
    m = jnp.mean(x, axis=axis, keepdims=True)
    v = jnp.var(x, axis=axis, keepdims=True)
    return (x - m) / jnp.sqrt(v + eps)

def _scatter_add(tgt, idx, src, axis=0):
    return tgt.at[idx].add(src)

def _segment_sum(src, seg, n):
    return jax.ops.segment_sum(src, seg, n)
kernel_name = 'mk_gnn_resnorm_d1_gnn_r64_c46587'

def setup_inputs(seed: int=0):
    np.random.seed(seed)
    _w = jnp.asarray

    def _rec_inputs():
        import jax
        import jax.numpy as jnp
        _gk = jax.random.key(seed)
        x = -0.0003713 + 1 * jax.random.normal(jax.random.fold_in(_gk, 1), (100000, 128), jnp.float32)
        src = jax.random.randint(jax.random.fold_in(_gk, 2), (50000,), 0, 100000, jnp.int32)
        dst = jnp.minimum((100000 * jax.random.uniform(jax.random.fold_in(_gk, 3), (50000,)) ** 2.0).astype(jnp.int32), 99999)
        _o = jnp.argsort(dst, stable=True)
        src = src[_o]
        dst = dst[_o]
        edge_attr_48 = -4.21973e-05 + 0.999841 * jax.random.normal(jax.random.fold_in(_gk, 11), (50000, 48), jnp.float32)
        return (x, src, dst, edge_attr_48)
    x, src, dst, edge_attr_48 = _rec_inputs()

    def _L0_gnn_setup():
        import jax, jax.numpy as jnp
        import numpy as np
        N_NODES = 100000
        N_EDGES = 25000
        NODE_DIM = 128
        EDGE_DIM = 48
        HID = 256
        OUT_DIM = 128
        IN_DIM = NODE_DIM + EDGE_DIM
        key = jax.random.key(seed)
        ks = jax.random.split(key, 10)

        def glorot(k, fan_in, fan_out):
            s = (6.0 / (fan_in + fan_out)) ** 0.5
            return jax.random.uniform(k, (fan_in, fan_out), jnp.float32, -s, s)
        return {'x': jax.random.normal(ks[0], (N_NODES, NODE_DIM), jnp.float32), 'edge_attr': jax.random.normal(ks[1], (N_EDGES, EDGE_DIM), jnp.float32), 'edge_index': jax.random.randint(ks[2], (2, N_EDGES), 0, N_NODES, jnp.int64), 'W1': glorot(ks[3], IN_DIM, HID), 'b1': jnp.zeros((HID,), jnp.float32), 'W2': glorot(ks[4], HID, HID), 'b2': jnp.zeros((HID,), jnp.float32), 'W3': glorot(ks[5], HID, OUT_DIM), 'b3': jnp.zeros((OUT_DIM,), jnp.float32)}
    _L0_gnn_all = _L0_gnn_setup()
    _L0_gnn_in = {k: v for k, v in _L0_gnn_all.items() if k in ('W1', 'b1', 'W2', 'b2', 'W3', 'b3')}
    del _L0_gnn_all
    return {'x': x, 'src': src, 'dst': dst, 'edge_attr_48': edge_attr_48, 'L0_gnn_W1': _L0_gnn_in['W1'], 'L0_gnn_b1': _L0_gnn_in['b1'], 'L0_gnn_W2': _L0_gnn_in['W2'], 'L0_gnn_b2': _L0_gnn_in['b2'], 'L0_gnn_W3': _L0_gnn_in['W3'], 'L0_gnn_b3': _L0_gnn_in['b3']}

def reference(x, src, dst, edge_attr_48, L0_gnn_W1, L0_gnn_b1, L0_gnn_W2, L0_gnn_b2, L0_gnn_W3, L0_gnn_b3):
    import jax
    import jax.numpy as jnp

    def _L0_gnn_ref(x, edge_attr, edge_index, W1, b1, W2, b2, W3, b3):
        import jax, jax.numpy as jnp
        import numpy as np
        N_NODES = 100000
        N_EDGES = 25000
        NODE_DIM = 128
        EDGE_DIM = 48
        HID = 256
        OUT_DIM = 128
        IN_DIM = NODE_DIM + EDGE_DIM
        r_idx = edge_index[1]
        agg_edge = jax.ops.segment_sum(edge_attr, r_idx, num_segments=N_NODES)
        collected = jnp.concatenate([x, agg_edge], axis=1)
        h = jax.nn.silu(collected @ W1 + b1)
        h = jax.nn.silu(h @ W2 + b2)
        delta_u = h @ W3 + b3
        new_u = x[:, -OUT_DIM:] + delta_u
        x_ = jnp.concatenate([x[:, :-OUT_DIM], new_u], axis=-1)
        return x_
    edge_index = jnp.stack([src, dst])
    x = _layernorm(x + _L0_gnn_ref(x, edge_attr_48, edge_index, L0_gnn_W1, L0_gnn_b1, L0_gnn_W2, L0_gnn_b2, L0_gnn_W3, L0_gnn_b3), axis=-1)
    return x

_drawn_inputs = setup_inputs


def setup_inputs(seed=0):
    import zlib

    import numpy as np

    out = dict(_drawn_inputs(seed))
    spreads = {'L0_gnn_b1': (0.0, 0.395), 'L0_gnn_b2': (0.0, 0.1), 'L0_gnn_b3': (0.0, 0.1)}
    factors = {}
    for name, (base, spread) in spreads.items():
        noise = np.random.default_rng([zlib.crc32(name.encode()), seed]).standard_normal(out[name].shape)
        drawn = base * np.exp(spread * noise) if base else spread * noise
        out[name] = jnp.asarray(drawn.astype(out[name].dtype))
    for name, factor in factors.items():
        out[name] = (out[name] * factor).astype(out[name].dtype)
    return out
```

```python
from contextlib import ExitStack

import numpy as np

import concourse.bass as bass
from concourse import mybir

F32 = mybir.dt.float32
F32R = mybir.dt.float32r
I32 = mybir.dt.int32
ALU = mybir.AluOpType
ACT = mybir.ActivationFunctionType
AX_X = mybir.AxisListType.X

NODE_DIM = 128
EDGE_DIM = 48
HID = 256
HALVES = HID // 128
NODES_P = 125
NODES_J = 4
GROUP = NODES_P * NODES_J
RING = 8
AGG_RING = 4
OUT_RING = 4
LAG = 8
NORM_BATCH = 4
EDGE_TILE = 125
CHUNK = 8
TILE_STRIDE = 3
IN_FLIGHT = 3
EPS = 1e-5


class Step:

    def __init__(self, ring_no, off, groups):
        self.ring_no, self.off, self.groups = ring_no, off, groups
        self.in_loop = not isinstance(ring_no, int)

    def has(self, k):
        return self.in_loop or 0 <= self.ring_no * RING + self.off + k < self.groups

    def done(self, k, per=1, plus=None):
        plus = per if plus is None else plus
        return self.ring_no * (RING * per) + ((self.off + k) * per + plus)

    def slot(self, k, ring=RING):
        return (self.off + k) % ring

    def landed(self, k, ring=RING):
        return self.ring_no * (16 * RING // ring) + 16 * ((self.off + k) // ring + 1)

    def group(self, k):
        return self.ring_no * RING + (self.off + k)


def build_gnn(nc, xT, edge_rows, target_cols, target_rows, W1, b1, W2, b2, W3, b3, out):
    groups = xT.shape[0]
    nodes = groups * GROUP
    tiles = edge_rows.shape[1]
    chunks = tiles // CHUNK
    quarter = tiles // 4
    spare_rows = CHUNK * EDGE_TILE
    g_half = groups // 2
    assert edge_rows.shape[0] == EDGE_TILE and tiles % CHUNK == 0 and tiles % 4 == 0 and quarter <= 128
    assert groups % RING == 0 and groups >= 4 * RING and g_half <= 128 and chunks % 2 == 0

    with ExitStack() as ctx:
        def sb(name, shape, dt=F32):
            return ctx.enter_context(nc.sbuf_tensor(name, shape, dt))

        def sem(name):
            return ctx.enter_context(nc.semaphore(name))

        table = nc.dram_tensor("node_sums", (nodes + spare_rows, EDGE_DIM), F32, kind="Internal").ap()

        ident = sb("ident", [128, 128])
        lower = sb("lower", [EDGE_TILE, EDGE_TILE])
        zeros_n = nodes * EDGE_DIM // 128
        zero_cols = next(c for c in range(2000, 0, -1) if zeros_n % c == 0)
        w1x_raw = sb("w1x_raw", [128, HID])
        w1e_raw = sb("w1e_raw", [2 * EDGE_DIM, HID])
        w2_raw = sb("w2_raw", [128, HALVES, HID])
        w3_raw = sb("w3_raw", [128, HALVES, NODE_DIM])
        w1x_hi, w1x_lo = sb("w1x_hi", [128, HID], F32R), sb("w1x_lo", [128, HID], F32R)
        w1e_hi, w1e_lo = sb("w1e_hi", [2 * EDGE_DIM, HID], F32R), sb("w1e_lo", [2 * EDGE_DIM, HID], F32R)
        w2_hi, w2_lo = sb("w2_hi", [128, HALVES, HID], F32R), sb("w2_lo", [128, HALVES, HID], F32R)
        w3_hi, w3_lo = sb("w3_hi", [128, HALVES, NODE_DIM], F32R), sb("w3_lo", [128, HALVES, NODE_DIM], F32R)
        b1_col, b2_col = sb("b1_col", [128, HALVES]), sb("b2_col", [128, HALVES])
        b3_col, b3_half = sb("b3_col", [128, 1]), sb("b3_half", [128, 1])

        edges = sb("edges", [EDGE_TILE, tiles, EDGE_DIM])
        targets = sb("targets", [EDGE_TILE, tiles], I32)
        targets_by_tile = sb("targets_by_tile", [quarter, 4, EDGE_TILE], I32)
        scatter_rows = sb("scatter_rows", [EDGE_TILE, tiles], I32)
        spare = sb("spare", [EDGE_TILE, CHUNK])
        t_col = sb("t_col", [EDGE_TILE, 2, CHUNK])
        n_match = sb("n_match", [EDGE_TILE, 2, CHUNK])
        to_spare = sb("to_spare", [EDGE_TILE, 2, CHUNK])
        go_spare = sb("go_spare", [EDGE_TILE, 2, CHUNK])
        sums_out = sb("sums_out", [EDGE_TILE, 2, CHUNK, EDGE_DIM])
        rows_out = sb("rows_out", [EDGE_TILE, 2, CHUNK], I32)
        tile_min, tile_max = sb("tile_min", [quarter, 4]), sb("tile_max", [quarter, 4])
        conflict = sb("conflict", [1, tiles], I32)
        tile_no = sb("tile_no", [quarter, 4])
        group_end = sb("group_end", [quarter, groups])
        reach_max = sb("reach_max", [quarter, groups])
        need_col = sb("need_col", [g_half, 2])
        tiles_needed = sb("tiles_needed", [1, groups], I32)

        x_in = sb("x_in", [128, RING, GROUP])
        x_hi, x_lo = sb("x_hi", [128, 2, GROUP], F32R), sb("x_lo", [128, 2, GROUP], F32R)
        agg_in = sb("agg_in", [NODES_P, AGG_RING, NODES_J, EDGE_DIM])
        agg_hl = sb("agg_hl", [NODES_P, 2, NODES_J, 2, EDGE_DIM])
        aggT = sb("aggT", [2 * EDGE_DIM, 2, GROUP], F32R)
        h1, h2 = sb("h1", [128, HALVES, GROUP]), sb("h2", [128, HALVES, GROUP])
        h1_hi, h1_lo = sb("h1_hi", [128, 2, HALVES, GROUP], F32R), sb("h1_lo", [128, 2, HALVES, GROUP], F32R)
        h2_hi, h2_lo = sb("h2_hi", [128, 2, HALVES, GROUP], F32R), sb("h2_lo", [128, 2, HALVES, GROUP], F32R)
        yT = sb("yT", [128, 2, GROUP])
        y_rows = sb("y_rows", [NODES_P, RING, NODES_J, NODE_DIM])
        stats = sb("stats", [NODES_P, RING, NODES_J, 6])
        n_stat = NORM_BATCH * NODES_J
        st = sb("st", [NODES_P, 8, n_stat])
        mean, rstd = sb("mean", [NODES_P, 2, n_stat]), sb("rstd", [NODES_P, 2, n_stat])
        out_rows = sb("out_rows", [128, OUT_RING, NODES_J, NODE_DIM])

        def within(tensor, at, p, shape):
            n = int(np.prod(shape))
            dims = "a b c d"[:2 * len(shape) - 1]
            return tensor[0:p, at:at + n].rearrange(f"q ({dims}) -> q {dims}",
                                                  **dict(zip(dims.split()[1:], shape[1:])))

        y_flat = y_rows[:].rearrange("p g j c -> p (g j c)")
        x_flat = x_in[:].rearrange("p g n -> p (g n)")
        t_row = within(y_flat, 0, EDGE_TILE, (2, CHUNK, EDGE_TILE))
        match = within(y_flat, 2 * CHUNK * EDGE_TILE, EDGE_TILE, (2, CHUNK, EDGE_TILE))
        min_row, max_row = within(x_flat, 0, 1, (tiles,)), within(x_flat, tiles, 1, (tiles,))
        below, above, overlap = (within(x_flat, (2 + 2 * k) * tiles, 1, (2, tiles)) for k in range(3))
        reach = within(x_flat, 8 * tiles, quarter, (4, groups))
        zeros = out_rows[:].rearrange("p g j c -> p (g j c)")

        bank = [ctx.enter_context(nc.psum_tensor(f"bank{i}", [128, 512], F32)) for i in range(7)]
        l1_ps, l2_ps = bank[0:2], bank[2:4]
        l3_ps, yT_ps, aggT_ps = bank[4], bank[5], bank[6]
        t_row_ps, sums_ps = bank[0:2], bank[2:4]

        ident_made, lower_made, consts_made = sem("ident_made"), sem("lower_made"), sem("consts_made")
        zeros_made, table_zeroed = sem("zeros_made"), sem("table_zeroed")
        targets_landed, by_tile_landed = sem("targets_landed"), sem("by_tile_landed")
        weights_landed, weights_split = sem("weights_landed"), sem("weights_split")
        ranges_done, ranges_rowed, flags_done = sem("ranges_done"), sem("ranges_rowed"), sem("flags_done")
        reach_done, reach_rowed, need_done, need_rowed, needs_ready = (
            sem("reach_done"), sem("reach_rowed"), sem("need_done"), sem("need_rowed"), sem("needs_ready"))
        dve_setup = sem("dve_setup")
        edges_landed = [sem(f"edges_landed{b}") for b in range(2)]
        staged, spread, t_row_ready = sem("staged"), sem("spread"), sem("t_row_ready")
        matched, summed, sums_stored = sem("matched"), sem("summed"), sem("sums_stored")
        spare_chosen, rows_ready, copied_out = sem("spare_chosen"), sem("rows_ready"), sem("copied_out")
        scattered = [sem(f"scattered{u}") for u in range(CHUNK)]
        tiles_landed = sem("tiles_landed")
        x_landed = [sem(f"x_landed{r}") for r in range(RING)]
        agg_landed = [sem(f"agg_landed{r}") for r in range(AGG_RING)]
        out_stored = [sem(f"out_stored{r}") for r in range(OUT_RING)]
        agg_hi_ready, agg_split, aggT_done, aggT_ready = (
            sem("agg_hi_ready"), sem("agg_split"), sem("aggT_done"), sem("aggT_ready"))
        x_hi_ready, x_lo_ready = sem("x_hi_ready"), sem("x_lo_ready")
        l1_done, h1_ready, h1_hi_ready, h1_lo_ready = (
            sem("l1_done"), sem("h1_ready"), sem("h1_hi_ready"), sem("h1_lo_ready"))
        l2_done, h2_ready, h2_hi_ready, h2_lo_ready = (
            sem("l2_done"), sem("h2_ready"), sem("h2_hi_ready"), sem("h2_lo_ready"))
        l3_done, yT_ready, y_turned, y_rows_ready = (
            sem("l3_done"), sem("yT_ready"), sem("y_turned"), sem("y_rows_ready"))
        stats_ready, norm_chain, norm_done = sem("stats_ready"), sem("norm_chain"), sem("norm_done")

        zero_dmas = zeros_n // zero_cols + 1
        front = [Step(0, s, groups) for s in range(-4, 2 * RING)]
        tail = [Step(0, s, groups) for s in range(groups - RING, groups + LAG)]

        def node_steps(eng, step):
            for s in front:
                step(s)
            with eng.Fori(2, groups // RING - 1) as i:
                for off in range(RING):
                    step(Step(i, off, groups))
            for s in tail:
                step(s)

        block = ctx.enter_context(nc.Block())

        @block.sync
        def _(sp):
            sp.dma_start(targets_by_tile[:], target_rows).then_inc(by_tile_landed, 16)
            sp.dma_start(targets[:], target_cols).then_inc(targets_landed, 16)

            def load_edges(c, b):
                sp.dma_start(edges[:, bass.ds(c * CHUNK, CHUNK), :],
                             edge_rows[:, bass.ds(c * CHUNK, CHUNK), :]).then_inc(edges_landed[b], 16)

            load_edges(0, 0)
            load_edges(1, 1)
            for dst, src in ((w1x_raw[:], W1[0:NODE_DIM, :]),
                             (w1e_raw[0:EDGE_DIM, :], W1[NODE_DIM:, :]),
                             (w1e_raw[EDGE_DIM:, :], W1[NODE_DIM:, :]),
                             (w2_raw[:], W2.rearrange("(t p) n -> p t n", p=128)),
                             (w3_raw[:], W3.rearrange("(t p) n -> p t n", p=128)),
                             (b1_col[:], b1), (b2_col[:], b2), (b3_col[:], b3)):
                sp.dma_start(dst, src).then_inc(weights_landed, 16)
            with sp.Fori(1, chunks // 2) as i:
                for b in range(2):
                    sp.wait_ge(edges_landed[b], 16 * i)
                    load_edges(2 * i + b, b)

            sp.wait_ge(needs_ready, 1)

            def step(s):
                if s.has(3):
                    if s.has(3 - RING):
                        sp.wait_ge(yT_ready, s.done(3 - RING))
                    sp.dma_start(x_in[:, s.slot(3), :],
                                 xT[bass.ds(s.group(3), 1), :, :].rearrange("g p n -> p (g n)"))\
                        .then_inc(x_landed[s.slot(3)], 16)
                if s.has(4):
                    if s.has(4 - AGG_RING):
                        sp.wait_ge(agg_split, s.done(4 - AGG_RING))
                    need = sp.value_load(tiles_needed[0:1, bass.ds(s.group(4), 1)], min_val=1, max_val=tiles)
                    sp.wait_ge(tiles_landed, need)
                    sp.dma_start(agg_in[:, s.slot(4, AGG_RING), :, :].rearrange("p j c -> p (j c)"),
                                 table[bass.ds(s.group(4) * GROUP, GROUP), :]
                                 .rearrange("(p j) c -> p (j c)", j=NODES_J))\
                        .then_inc(agg_landed[s.slot(4, AGG_RING)], 16)
                if s.has(-LAG):
                    sp.wait_ge(norm_done, s.done(-LAG))
                    sp.dma_start(out[bass.ds(s.group(-LAG) * GROUP, GROUP), :]
                                 .rearrange("(p j) c -> p (j c)", j=NODES_J),
                                 out_rows[0:NODES_P, s.slot(-LAG, OUT_RING), :, :].rearrange("p j c -> p (j c)"))\
                        .then_inc(out_stored[s.slot(-LAG, OUT_RING)], 16)

            node_steps(sp, step)
            for r in range(OUT_RING):
                sp.wait_ge(out_stored[r], 16 * (groups // OUT_RING))

        @block.gpsimd
        def _(pool):
            nc.gpsimd.memset(ident[:], 0.0).then_inc(ident_made, 1)
            nc.gpsimd.memset(lower[:], 1.0).then_inc(lower_made, 1)
            pool.wait_ge(ident_made, 1)
            nc.gpsimd.affine_select(out=ident[:], in_=ident[:], compare_op=ALU.not_equal, fill=1.0, base=0,
                                    pattern=[[-1, 128]], channel_multiplier=1).then_inc(ident_made, 1)
            pool.wait_ge(lower_made, 1)
            nc.gpsimd.affine_select(out=lower[:], in_=lower[:], compare_op=ALU.is_ge, fill=0.0, base=0,
                                    pattern=[[-1, EDGE_TILE]], channel_multiplier=1).then_inc(lower_made, 1)
            nc.gpsimd.iota(spare[:], [[EDGE_TILE, CHUNK]], base=nodes, channel_multiplier=1,
                           allow_small_or_imprecise_dtypes=True).then_inc(consts_made, 1)
            nc.gpsimd.iota(tile_no[:], [[quarter, 4]], base=1, channel_multiplier=1,
                           allow_small_or_imprecise_dtypes=True).then_inc(consts_made, 1)
            nc.gpsimd.iota(group_end[:], [[GROUP, groups]], base=GROUP, channel_multiplier=0,
                           allow_small_or_imprecise_dtypes=True).then_inc(consts_made, 1)

            pool.wait_ge(flags_done, 1)
            pool.wait_ge(table_zeroed, 16 * zero_dmas)

            def landed(c, u, back):
                v = u - back
                pool.wait_ge(scattered[v % CHUNK], 16 * (c + v // CHUNK + 1))

            def scatter_chunk(c, b, first=False):
                pool.wait_ge(sums_stored, c + 1)
                nc.gpsimd.tensor_copy(sums_out[:, b, :, :].rearrange("p u c -> p (u c)"),
                                      edges[:, bass.ds(c * CHUNK, CHUNK), :].rearrange("p u c -> p (u c)"))\
                    .then_inc(copied_out, 1)
                pool.wait_ge(rows_ready, c + 1)
                nc.gpsimd.tensor_copy(rows_out[:, b, :], scatter_rows[:, bass.ds(c * CHUNK, CHUNK)])\
                    .then_inc(copied_out, 1)
                pool.wait_ge(copied_out, 2 * c + 2)
                for u in range(CHUNK):
                    if not first or u >= IN_FLIGHT:
                        landed(c, u, IN_FLIGHT)
                        pool.sem_inc(tiles_landed, 1)
                    if not first or u > 0:
                        flag = pool.value_load(conflict[0:1, bass.ds(c * CHUNK + u, 1)], min_val=0, max_val=1)
                        with pool.If(flag > 0):
                            for back in range(1, IN_FLIGHT):
                                if not first or u >= back:
                                    landed(c, u, back)
                    nc.gpsimd.indirect_dma_start(
                        table, bass.IndirectOffsetOnAxis(ap=rows_out[:, b, u:u + 1], axis=0),
                        sums_out[:, b, u, :], None, bounds_check=nodes + spare_rows - 1, oob_is_err=True,
                        compute_op=ALU.add).then_inc(scattered[u], 16)

            scatter_chunk(0, 0, first=True)
            scatter_chunk(1, 1)
            with pool.Fori(1, chunks // 2) as i:
                for b in range(2):
                    scatter_chunk(2 * i + b, b)
            for u in range(IN_FLIGHT):
                landed(chunks, u, IN_FLIGHT)
                pool.sem_inc(tiles_landed, 1)

        @block.tensor
        def _(pe):
            pe.wait_ge(ident_made, 2)

            pe.wait_ge(ranges_done, 2)
            for c in range(4):
                nc.tensor.matmul(bank[4][0:1, c * quarter:(c + 1) * quarter], tile_min[:, c:c + 1],
                                 ident[0:quarter, 0:quarter], start=True, stop=True)
                last = nc.tensor.matmul(bank[5][0:1, c * quarter:(c + 1) * quarter], tile_max[:, c:c + 1],
                                        ident[0:quarter, 0:quarter], start=True, stop=True)
            last.then_inc(ranges_rowed, 1)

            def spread_targets(c, b):
                pe.wait_ge(staged, c + 1)
                for n in range(2):
                    if not isinstance(c, int) or c > 0:
                        pe.wait_ge(t_row_ready, 2 * c + n - 1)
                    for v in range(4):
                        u = 4 * n + v
                        last = nc.tensor.transpose(
                            t_row_ps[n][0:EDGE_TILE, v * EDGE_TILE:(v + 1) * EDGE_TILE],
                            t_col[:, b, u:u + 1].to_broadcast([EDGE_TILE, EDGE_TILE]),
                            ident[0:EDGE_TILE, 0:EDGE_TILE])
                    last.then_inc(spread, 1)

            def sum_chunk(c, b, i):
                pe.wait_ge(edges_landed[b], 16 * (i + 1))
                if not isinstance(c, int) or c > 1:
                    pe.wait_ge(sums_stored, c - 1)
                for u in range(CHUNK):
                    pe.wait_ge(matched, c * CHUNK + u + 1)
                    last = nc.tensor.matmul(
                        sums_ps[b][0:EDGE_TILE, u * EDGE_DIM:(u + 1) * EDGE_DIM], match[:, b, u, :],
                        edges[:, bass.ds(c * CHUNK + u, 1), :].rearrange("p u c -> p (u c)"),
                        start=True, stop=True)
                last.then_inc(summed, 1)

            spread_targets(0, 0)
            spread_targets(1, 1)
            sum_chunk(0, 0, 0)
            spread_targets(2, 0)
            sum_chunk(1, 1, 0)
            with pe.Fori(1, chunks // 2 - 1) as i:
                spread_targets(2 * i + 1, 1)
                sum_chunk(2 * i, 0, i)
                spread_targets(2 * i + 2, 0)
                sum_chunk(2 * i + 1, 1, i)
            spread_targets(chunks - 1, 1)
            sum_chunk(chunks - 2, 0, chunks // 2 - 1)
            sum_chunk(chunks - 1, 1, chunks // 2 - 1)

            pe.wait_ge(reach_done, 1)
            for h in range(2):
                last = nc.tensor.matmul(bank[4 + h][0:g_half, 0:quarter], reach_max[:, h * g_half:(h + 1) * g_half],
                                        ident[0:quarter, 0:quarter], start=True, stop=True)
            last.then_inc(reach_rowed, 1)
            pe.wait_ge(need_done, 2)
            for h in range(2):
                last = nc.tensor.matmul(bank[6][0:1, h * g_half:(h + 1) * g_half], need_col[:, h:h + 1],
                                        ident[0:g_half, 0:g_half], start=True, stop=True)
            last.then_inc(need_rowed, 1)

            pe.wait_ge(weights_split, 1)
            pe.wait_ge(t_row_ready, 2 * chunks)
            pe.wait_ge(sums_stored, chunks)
            pe.wait_ge(needs_ready, 1)

            def step(s):
                if s.has(0):
                    d = s.off % 2
                    pe.wait_ge(x_lo_ready, s.done(0))
                    pe.wait_ge(aggT_ready, s.done(0))
                    for m in range(HALVES):
                        cols = slice(m * 128, (m + 1) * 128)
                        if s.has(-1):
                            pe.wait_ge(h1_ready, s.done(-1, per=2, plus=m + 1))
                        o = l1_ps[m][:, 0:GROUP]
                        nc.tensor.matmul(o, w1x_hi[:, cols], x_hi[:, d, :], start=True, stop=False)
                        nc.tensor.matmul(o, w1x_hi[:, cols], x_lo[:, d, :], start=False, stop=False)
                        nc.tensor.matmul(o, w1x_lo[:, cols], x_hi[:, d, :], start=False, stop=False)
                        nc.tensor.matmul(o, w1e_hi[:, cols], aggT[:, d, :], start=False, stop=False)
                        nc.tensor.matmul(o, w1e_lo[:, cols], aggT[:, d, :], start=False, stop=True)\
                            .then_inc(l1_done, 1)
                if s.has(1):
                    d = (s.off + 1) % 2
                    pe.wait_ge(agg_split, s.done(1))
                    if s.has(0):
                        pe.wait_ge(aggT_ready, s.done(0))
                    for j in range(NODES_J):
                        last = nc.tensor.transpose(
                            aggT_ps[0:2 * EDGE_DIM, j * NODES_P:(j + 1) * NODES_P],
                            agg_hl[:, d, j, :, :].rearrange("p h c -> p (h c)"),
                            ident[0:NODES_P, 0:NODES_P])
                    last.then_inc(aggT_done, 1)
                if s.has(-2):
                    d = s.off % 2
                    o = l3_ps[:, 0:GROUP]
                    if s.has(-3):
                        pe.wait_ge(yT_ready, s.done(-3))
                    for t in range(HALVES):
                        pe.wait_ge(h2_lo_ready, s.done(-2, per=2, plus=t + 1))
                        nc.tensor.matmul(o, w3_hi[:, t, :], h2_hi[:, d, t, :], start=(t == 0), stop=False)
                        nc.tensor.matmul(o, w3_hi[:, t, :], h2_lo[:, d, t, :], start=False, stop=False)
                        last = nc.tensor.matmul(o, w3_lo[:, t, :], h2_hi[:, d, t, :], start=False,
                                                stop=(t == HALVES - 1))
                    last.then_inc(l3_done, 1)
                if s.has(-1):
                    d = (s.off - 1) % 2
                    pe.wait_ge(h1_lo_ready, s.done(-1))
                    for m in range(HALVES):
                        cols = slice(m * 128, (m + 1) * 128)
                        if s.has(-2):
                            pe.wait_ge(h2_ready, s.done(-2, per=2, plus=m + 1))
                        o = l2_ps[m][:, 0:GROUP]
                        for t in range(HALVES):
                            nc.tensor.matmul(o, w2_hi[:, t, cols], h1_hi[:, d, t, :], start=(t == 0), stop=False)
                            nc.tensor.matmul(o, w2_hi[:, t, cols], h1_lo[:, d, t, :], start=False, stop=False)
                            last = nc.tensor.matmul(o, w2_lo[:, t, cols], h1_hi[:, d, t, :], start=False,
                                                    stop=(t == HALVES - 1))
                        last.then_inc(l2_done, 1)
                if s.has(-3):
                    d = (s.off - 3) % 2
                    pe.wait_ge(yT_ready, s.done(-3))
                    if s.has(-4):
                        pe.wait_ge(y_rows_ready, s.done(-4))
                    for j in range(NODES_J):
                        last = nc.tensor.transpose(yT_ps[0:NODES_P, j * NODE_DIM:(j + 1) * NODE_DIM],
                                                   yT[:, d, j * NODES_P:(j + 1) * NODES_P], ident[:])
                    last.then_inc(y_turned, 1)

            node_steps(pe, step)

        @block.scalar
        def _(act):
            act.wait_ge(zeros_made, 1)
            flat = table.rearrange("n c -> (n c)")
            rows = flat[0:nodes * EDGE_DIM].rearrange("(p k z) -> k p z", p=128, z=zero_cols)
            for k in range(zero_dmas - 1):
                act.dma_start(rows[k], zeros[:, 0:zero_cols]).then_inc(table_zeroed, 16)
            n = spare_rows * EDGE_DIM // 128
            act.dma_start(flat[nodes * EDGE_DIM:].rearrange("(p z) -> p z", z=n), zeros[:, 0:n])\
                .then_inc(table_zeroed, 16)

            def copy_targets(c, b):
                for n in range(2):
                    act.wait_ge(spread, 2 * c + n + 1)
                    if not isinstance(c, int) or c > 1:
                        act.wait_ge(matched, (c - 2) * CHUNK + 4 * n + 4)
                    nc.scalar.activation(
                        t_row[:, b, 4 * n:4 * n + 4, :].rearrange("p u e -> p (u e)"),
                        t_row_ps[n][0:EDGE_TILE, 0:4 * EDGE_TILE], ACT.Copy).then_inc(t_row_ready, 1)

            def store_sums(c, b):
                act.wait_ge(summed, c + 1)
                nc.scalar.activation(
                    edges[:, bass.ds(c * CHUNK, CHUNK), :].rearrange("p u c -> p (u c)"),
                    sums_ps[b][0:EDGE_TILE, 0:CHUNK * EDGE_DIM], ACT.Copy).then_inc(sums_stored, 1)

            copy_targets(0, 0)
            copy_targets(1, 1)
            store_sums(0, 0)
            copy_targets(2, 0)
            store_sums(1, 1)
            with act.Fori(1, chunks // 2 - 1) as i:
                copy_targets(2 * i + 1, 1)
                store_sums(2 * i, 0)
                copy_targets(2 * i + 2, 0)
                store_sums(2 * i + 1, 1)
            copy_targets(chunks - 1, 1)
            store_sums(chunks - 2, 0)
            store_sums(chunks - 1, 1)

            act.wait_ge(weights_landed, 16 * 8)

            def step(s):
                if s.has(0):
                    d = s.off % 2
                    if s.has(-1):
                        act.wait_ge(h1_lo_ready, s.done(-1))
                    for m in range(HALVES):
                        act.wait_ge(l1_done, s.done(0, per=2, plus=m + 1))
                        nc.scalar.activation(h1[:, m, :], l1_ps[m][:, 0:GROUP], ACT.Silu,
                                             bias=b1_col[:, m:m + 1]).then_inc(h1_ready, 1)
                if s.has(1):
                    d = (s.off + 1) % 2
                    act.wait_ge(aggT_done, s.done(1))
                    if s.has(-1):
                        act.wait_ge(l1_done, s.done(-1, per=2))
                    nc.scalar.activation(aggT[:, d, :], aggT_ps[0:2 * EDGE_DIM, 0:GROUP], ACT.Copy)\
                        .then_inc(aggT_ready, 1)
                    act.wait_ge(x_landed[s.slot(1)], s.landed(1))
                    nc.scalar.activation(x_hi[:, d, :], x_in[:, s.slot(1), :], ACT.Copy).then_inc(x_hi_ready, 1)
                if s.has(0):
                    d = s.off % 2
                    act.wait_ge(h1_ready, s.done(0, per=2))
                    if s.has(-2):
                        act.wait_ge(l2_done, s.done(-2, per=2))
                    nc.scalar.activation(h1_hi[:, d, :, :].rearrange("p t n -> p (t n)"),
                                         h1[:].rearrange("p t n -> p (t n)"), ACT.Copy)\
                        .then_inc(h1_hi_ready, 1)
                if s.has(-1):
                    d = (s.off - 1) % 2
                    if s.has(-2):
                        act.wait_ge(h2_lo_ready, s.done(-2, per=2))
                    for m in range(HALVES):
                        act.wait_ge(l2_done, s.done(-1, per=2, plus=m + 1))
                        nc.scalar.activation(h2[:, m, :], l2_ps[m][:, 0:GROUP], ACT.Silu,
                                             bias=b2_col[:, m:m + 1]).then_inc(h2_ready, 1)
                if s.has(-3):
                    act.wait_ge(y_turned, s.done(-3))
                    if s.has(-3 - RING):
                        act.wait_ge(norm_done, s.done(-3 - RING))
                    nc.scalar.activation(y_rows[:, s.slot(-3), :, :].rearrange("p j c -> p (j c)"),
                                         yT_ps[0:NODES_P, :], ACT.Copy).then_inc(y_rows_ready, 1)

            node_steps(act, step)

        @block.vector
        def _(dve):
            nc.vector.memset(zeros[:, 0:zero_cols], 0.0).then_inc(zeros_made, 1)

            dve.wait_ge(by_tile_landed, 16)
            nc.vector.tensor_reduce(tile_min[:], targets_by_tile[:], AX_X, ALU.min).then_inc(ranges_done, 1)
            nc.vector.tensor_reduce(tile_max[:], targets_by_tile[:], AX_X, ALU.max).then_inc(ranges_done, 1)

            def stage(c, b):
                if not isinstance(c, int) or c > 1:
                    dve.wait_ge(spread, 2 * (c - 1))
                    dve.wait_ge(rows_ready, c - 1)
                nc.vector.tensor_copy(t_col[:, b, :], targets[:, bass.ds(c * CHUNK, CHUNK)]).then_inc(staged, 1)

            dve.wait_ge(targets_landed, 16)
            stage(0, 0)

            dve.wait_ge(ranges_rowed, 1)
            nc.vector.tensor_copy(min_row[:], bank[4][0:1, 0:tiles]).then_inc(dve_setup, 1)
            nc.vector.tensor_copy(max_row[:], bank[5][0:1, 0:tiles]).then_inc(dve_setup, 1)
            nc.vector.memset(overlap[:], 0.0).then_inc(dve_setup, 1)
            dve.wait_ge(dve_setup, 3)
            for n in range(2):
                back = n + 1
                nc.vector.tensor_tensor(below[:, n, back:], min_row[:, back:], max_row[:, :tiles - back], ALU.is_le)\
                    .then_inc(dve_setup, 1)
                nc.vector.tensor_tensor(above[:, n, back:], max_row[:, back:], min_row[:, :tiles - back], ALU.is_ge)\
                    .then_inc(dve_setup, 1)
            dve.wait_ge(dve_setup, 7)
            for n in range(2):
                back = n + 1
                nc.vector.tensor_tensor(overlap[:, n, back:], below[:, n, back:], above[:, n, back:], ALU.mult)\
                    .then_inc(dve_setup, 1)
            dve.wait_ge(dve_setup, 9)
            nc.vector.tensor_tensor(conflict[:], overlap[:, 0, :], overlap[:, 1, :], ALU.max).then_inc(flags_done, 1)

            dve.wait_ge(lower_made, 2)
            dve.wait_ge(consts_made, 3)

            def match_chunk(c, b):
                if not isinstance(c, int) or c > 1:
                    dve.wait_ge(summed, c - 1)
                for u in range(CHUNK):
                    if u % 4 == 0:
                        dve.wait_ge(t_row_ready, 2 * c + u // 4 + 1)
                    nc.vector.scalar_tensor_tensor(match[:, b, u, :], t_row[:, b, u, :], t_col[:, b, u:u + 1],
                                                   lower[:], ALU.is_equal, ALU.mult,
                                                   accum_out=n_match[:, b, u:u + 1]).then_inc(matched, 1)
                nc.vector.tensor_tensor(to_spare[:, b, :], spare[:], t_col[:, b, :], ALU.subtract)\
                    .then_inc(spare_chosen, 1)
                dve.wait_ge(matched, (c + 1) * CHUNK)
                dve.wait_ge(spare_chosen, 2 * c + 1)
                nc.vector.scalar_tensor_tensor(go_spare[:, b, :], n_match[:, b, :], 1.5, to_spare[:, b, :],
                                               ALU.is_gt, ALU.mult).then_inc(spare_chosen, 1)
                dve.wait_ge(spare_chosen, 2 * c + 2)
                nc.vector.tensor_tensor(scatter_rows[:, bass.ds(c * CHUNK, CHUNK)], go_spare[:, b, :],
                                        t_col[:, b, :], ALU.add).then_inc(rows_ready, 1)

            stage(1, 1)
            dve.wait_ge(staged, 2)
            match_chunk(0, 0)
            stage(2, 0)
            match_chunk(1, 1)
            with dve.Fori(1, chunks // 2 - 1) as i:
                stage(2 * i + 1, 1)
                match_chunk(2 * i, 0)
                stage(2 * i + 2, 0)
                match_chunk(2 * i + 1, 1)
            stage(chunks - 1, 1)
            match_chunk(chunks - 2, 0)
            dve.wait_ge(staged, chunks)
            match_chunk(chunks - 1, 1)

            for c in range(4):
                nc.vector.tensor_scalar(reach[:, c, :], group_end[:], tile_min[:, c:c + 1], tile_no[:, c:c + 1],
                                        ALU.is_gt, ALU.mult).then_inc(dve_setup, 1)
            dve.wait_ge(dve_setup, 13)
            nc.vector.tensor_reduce(reach_max[:], reach[:].rearrange("p c g -> p g c"), AX_X, ALU.max)\
                .then_inc(reach_done, 1)

            dve.wait_ge(weights_landed, 16 * 8)
            nc.vector.tensor_scalar(w3_raw[:], w3_raw[:], 0.5, None, ALU.mult).then_inc(dve_setup, 1)
            nc.vector.tensor_scalar(b3_half[:], b3_col[:], 0.5, None, ALU.mult).then_inc(dve_setup, 1)
            dve.wait_ge(dve_setup, 15)
            parts = ((w1x_raw, w1x_hi, w1x_lo), (w1e_raw, w1e_hi, w1e_lo), (w2_raw, w2_hi, w2_lo),
                     (w3_raw, w3_hi, w3_lo))
            for raw, hi, lo in parts:
                nc.vector.tensor_copy(hi[:], raw[:]).then_inc(dve_setup, 1)
            dve.wait_ge(dve_setup, 19)
            for raw, hi, lo in parts:
                last = nc.vector.tensor_tensor(lo[:], raw[:], hi[:].bitcast(F32), ALU.subtract)
            last.then_inc(weights_split, 1)

            dve.wait_ge(reach_rowed, 1)
            for h in range(2):
                nc.vector.tensor_reduce(need_col[:, h:h + 1], bank[4 + h][0:g_half, 0:quarter], AX_X, ALU.max)\
                    .then_inc(need_done, 1)
            dve.wait_ge(need_rowed, 1)
            nc.vector.tensor_scalar(tiles_needed[:], bank[6][0:1, 0:groups], 1.0, None, ALU.max)\
                .then_inc(needs_ready, 1)

            CHAIN = 18

            def norm_batch(s):
                q = (s.off // NORM_BATCH + 1) % 2
                first = q * NORM_BATCH
                view = stats[:, first:first + NORM_BATCH, :, :].rearrange("p g j f -> p (g j) f")
                mean_even, m2_even, mean_odd, m2_odd = (view[:, :, f] for f in (1, 2, 4, 5))
                n = [0]
                before = (s.ring_no * (RING // NORM_BATCH) + (s.off + 1) // NORM_BATCH - 2) * CHAIN

                def link(ins, wait=True):
                    n[0] += 1
                    ins.then_inc(norm_chain, 1)
                    if wait:
                        dve.wait_ge(norm_chain, before + n[0])

                tmp = [st[:, k, :] for k in range(8)]
                dve.wait_ge(stats_ready, s.done(-4))
                tt, stt, ts = nc.vector.tensor_tensor, nc.vector.scalar_tensor_tensor, nc.vector.tensor_scalar
                link(tt(tmp[0], mean_even, mean_odd, ALU.add), wait=False)
                link(tt(tmp[1], mean_even, mean_odd, ALU.subtract), wait=False)
                link(tt(tmp[2], m2_even, m2_odd, ALU.add))
                link(ts(mean[:, q, :], tmp[0], 0.5, None, ALU.mult), wait=False)
                link(tt(tmp[3], tmp[1], tmp[1], ALU.mult))
                link(stt(tmp[4], tmp[3], NODE_DIM / 4.0, tmp[2], ALU.mult, ALU.add))
                link(ts(tmp[5], tmp[4], 1.0 / NODE_DIM, EPS / 4.0, ALU.mult, ALU.add))
                link(ts(tmp[6].bitcast(I32), tmp[5].bitcast(I32), 1, None, ALU.logical_shift_right))
                link(ts(tmp[7].bitcast(I32), tmp[6].bitcast(I32), -1.0, float(0x5F3759DF), ALU.mult, ALU.add))
                y, other = tmp[7], tmp[6]
                for k in range(3):
                    link(tt(tmp[3], y, y, ALU.mult))
                    link(stt(tmp[4], tmp[3], -0.5, tmp[5], ALU.mult, ALU.mult))
                    target = rstd[:, q, :] if k == 2 else other
                    link(stt(target, tmp[4], 1.5, y, ALU.add, ALU.mult))
                    y, other = other, y
                assert n[0] == CHAIN

            def step(s):
                if s.has(-4):
                    dve.wait_ge(y_rows_ready, s.done(-4))
                    for j in range(NODES_J):
                        last = nc.vector.bn_stats(stats[:, s.slot(-4), j, :], y_rows[:, s.slot(-4), j, :])
                    last.then_inc(stats_ready, 1)
                if s.has(-LAG):
                    q = (s.off // NORM_BATCH) % 2
                    if s.has(-LAG - OUT_RING):
                        dve.wait_ge(out_stored[s.slot(-LAG, OUT_RING)], s.landed(-LAG - OUT_RING, OUT_RING))
                    for j in range(NODES_J):
                        k = (s.off % NORM_BATCH) * NODES_J + j
                        last = nc.vector.tensor_scalar(out_rows[0:NODES_P, s.slot(-LAG, OUT_RING), j, :], y_rows[:, s.slot(-LAG), j, :],
                                                       mean[:, q, k:k + 1], rstd[:, q, k:k + 1],
                                                       ALU.subtract, ALU.mult)
                    last.then_inc(norm_done, 1)
                if s.off % NORM_BATCH == NORM_BATCH - 1 and s.has(-4):
                    norm_batch(s)
                if s.has(2):
                    d = s.off % 2
                    dve.wait_ge(agg_landed[s.slot(2, AGG_RING)], s.landed(2, AGG_RING))
                    if s.has(0):
                        dve.wait_ge(aggT_done, s.done(0))
                    nc.vector.tensor_copy(agg_hl[:, d, :, 0, :].bitcast(F32R), agg_in[:, s.slot(2, AGG_RING), :, :])\
                        .then_inc(agg_hi_ready, 1)
                    dve.wait_ge(agg_hi_ready, s.done(2))
                    nc.vector.tensor_tensor(agg_hl[:, d, :, 1, :], agg_in[:, s.slot(2, AGG_RING), :, :],
                                            agg_hl[:, d, :, 0, :], ALU.subtract).then_inc(agg_split, 1)
                if s.has(1):
                    d = (s.off + 1) % 2
                    dve.wait_ge(x_hi_ready, s.done(1))
                    nc.vector.tensor_tensor(x_lo[:, d, :], x_in[:, s.slot(1), :], x_hi[:, d, :].bitcast(F32),
                                            ALU.subtract).then_inc(x_lo_ready, 1)
                if s.has(0):
                    d = s.off % 2
                    dve.wait_ge(h1_hi_ready, s.done(0))
                    nc.vector.tensor_tensor(h1_lo[:, d, :, :].rearrange("p t n -> p (t n)"),
                                            h1[:].rearrange("p t n -> p (t n)"),
                                            h1_hi[:, d, :, :].rearrange("p t n -> p (t n)").bitcast(F32),
                                            ALU.subtract).then_inc(h1_lo_ready, 1)
                if s.has(-2):
                    d = s.off % 2
                    dve.wait_ge(l3_done, s.done(-2))
                    if s.has(-4):
                        dve.wait_ge(y_turned, s.done(-4))
                    nc.vector.scalar_tensor_tensor(yT[:, d, :], l3_ps[:, 0:GROUP], b3_half[:],
                                                   x_in[:, s.slot(-2), :], ALU.add, ALU.add)\
                        .then_inc(yT_ready, 1)
                if s.has(-1):
                    d = (s.off - 1) % 2
                    if s.has(-3):
                        dve.wait_ge(l3_done, s.done(-3))
                    for m in range(HALVES):
                        dve.wait_ge(h2_ready, s.done(-1, per=2, plus=m + 1))
                        nc.vector.tensor_copy(h2_hi[:, d, m, :], h2[:, m, :]).then_inc(h2_hi_ready, 1)
                        dve.wait_ge(h2_hi_ready, s.done(-1, per=2, plus=m + 1))
                        nc.vector.tensor_tensor(h2_lo[:, d, m, :], h2[:, m, :], h2_hi[:, d, m, :].bitcast(F32),
                                                ALU.subtract).then_inc(h2_lo_ready, 1)

            node_steps(dve, step)


def kernel(x, src, dst, edge_attr_48, L0_gnn_W1, L0_gnn_b1, L0_gnn_W2, L0_gnn_b2, L0_gnn_W3, L0_gnn_b3):
    import concourse.bacc as bacc
    from concourse.bass_utils import run_bass_kernel_spmd

    x = np.asarray(x)
    nodes = x.shape[0]
    groups = nodes // GROUP
    tiles = np.shape(dst)[0] // EDGE_TILE
    order = np.array([k // CHUNK * CHUNK + k * TILE_STRIDE % CHUNK for k in range(tiles)])
    by_tile = np.asarray(dst).reshape(tiles, EDGE_TILE)[order]
    arrays = {
        "xT": x.reshape(groups, NODES_P, NODES_J, NODE_DIM).transpose(0, 3, 2, 1).reshape(groups, NODE_DIM, GROUP),
        "edge_rows": np.asarray(edge_attr_48).reshape(tiles, EDGE_TILE, EDGE_DIM)[order].transpose(1, 0, 2),
        "target_cols": by_tile.T,
        "target_rows": by_tile.reshape(4, tiles // 4, EDGE_TILE).transpose(1, 0, 2),
        "W1": np.asarray(L0_gnn_W1),
        "b1": np.asarray(L0_gnn_b1).reshape(HALVES, 128).T,
        "W2": np.asarray(L0_gnn_W2),
        "b2": np.asarray(L0_gnn_b2).reshape(HALVES, 128).T,
        "W3": np.asarray(L0_gnn_W3),
        "b3": np.asarray(L0_gnn_b3).reshape(NODE_DIM, 1),
    }
    arrays = {name: np.ascontiguousarray(a) for name, a in arrays.items()}
    nc = bacc.Bacc("TRN2", target_bir_lowering=False, num_devices=1)
    args = [nc.dram_tensor(name, a.shape, mybir.dt.from_np(a.dtype), kind="ExternalInput").ap()
            for name, a in arrays.items()]
    out = nc.dram_tensor("out", (nodes, NODE_DIM), F32, kind="ExternalOutput").ap()
    build_gnn(nc, *args, out)
    r = run_bass_kernel_spmd(nc, [arrays], core_ids=[0])
    return r.results[0]["out"]
```

```python
from contextlib import ExitStack

import numpy as np

import concourse.bass as bass
from concourse import mybir

F32 = mybir.dt.float32
F32R = mybir.dt.float32r
I32 = mybir.dt.int32
ALU = mybir.AluOpType
ACT = mybir.ActivationFunctionType
AX_X = mybir.AxisListType.X

NODE_DIM = 128
EDGE_DIM = 48
HID = 256
HALVES = HID // 128
NODES_P = 125
NODES_J = 4
GROUP = NODES_P * NODES_J
RING = 8
AGG_RING = 4
OUT_RING = 4
LAG = 9
NORM_BATCH = 4
EDGE_TILE = 125
CHUNK = 8
TILE_STRIDE = 3
LO_ROWS = 64
IN_FLIGHT = 3
EPS = 1e-5


class Step:

    def __init__(self, ring_no, off, groups):
        self.ring_no, self.off, self.groups = ring_no, off, groups
        self.in_loop = not isinstance(ring_no, int)

    def has(self, k):
        return self.in_loop or 0 <= self.ring_no * RING + self.off + k < self.groups

    def done(self, k, per=1, plus=None):
        plus = per if plus is None else plus
        return self.ring_no * (RING * per) + ((self.off + k) * per + plus)

    def slot(self, k, ring=RING):
        return (self.off + k) % ring

    def landed(self, k, ring=RING):
        return self.ring_no * (16 * RING // ring) + 16 * ((self.off + k) // ring + 1)

    def group(self, k):
        return self.ring_no * RING + (self.off + k)


def build_gnn(nc, xT, edge_rows, target_cols, target_rows, W1, b1, W2, b2, W3, b3, out):
    groups = xT.shape[0]
    nodes = groups * GROUP
    tiles = edge_rows.shape[1]
    chunks = tiles // CHUNK
    spare_rows = CHUNK * EDGE_TILE
    g_half = groups // 2
    assert edge_rows.shape[0] == EDGE_TILE and tiles % CHUNK == 0 and chunks <= LO_ROWS
    assert groups % RING == 0 and groups >= 4 * RING and g_half <= 128 and chunks % 2 == 0 and chunks >= 8

    with ExitStack() as ctx:
        def sb(name, shape, dt=F32):
            return ctx.enter_context(nc.sbuf_tensor(name, shape, dt))

        def sem(name):
            return ctx.enter_context(nc.semaphore(name))

        table = nc.dram_tensor("node_sums", (nodes + spare_rows, EDGE_DIM), F32, kind="Internal").ap()

        ident = sb("ident", [128, 128])
        pick = sb("pick", [128, chunks])
        lower = sb("lower", [EDGE_TILE, EDGE_TILE])
        zeros_n = nodes * EDGE_DIM // 128
        zero_cols = next(c for c in range(2000, 0, -1) if zeros_n % (2 * c) == 0)
        w1x_raw = sb("w1x_raw", [128, HID])
        w1e_raw = sb("w1e_raw", [2 * EDGE_DIM, HID])
        w2_raw = sb("w2_raw", [128, HALVES, HID])
        w3_raw = sb("w3_raw", [128, HALVES, NODE_DIM])
        w1x_hi, w1x_lo = sb("w1x_hi", [128, HID], F32R), sb("w1x_lo", [128, HID], F32R)
        w1e_hi, w1e_lo = sb("w1e_hi", [2 * EDGE_DIM, HID], F32R), sb("w1e_lo", [2 * EDGE_DIM, HID], F32R)
        w2_hi, w2_lo = sb("w2_hi", [128, HALVES, HID], F32R), sb("w2_lo", [128, HALVES, HID], F32R)
        w3_hi, w3_lo = sb("w3_hi", [128, HALVES, NODE_DIM], F32R), sb("w3_lo", [128, HALVES, NODE_DIM], F32R)
        b1_col, b2_col = sb("b1_col", [128, HALVES]), sb("b2_col", [128, HALVES])
        b3_col, b3_half = sb("b3_col", [128, 1]), sb("b3_half", [128, 1])

        edges = sb("edges", [EDGE_TILE, tiles, EDGE_DIM])
        targets = sb("targets", [EDGE_TILE, tiles], I32)
        targets_by_chunk = sb("targets_by_chunk", [128, CHUNK, EDGE_TILE], I32)
        scatter_rows = sb("scatter_rows", [EDGE_TILE, tiles], I32)
        spare = sb("spare", [EDGE_TILE, CHUNK])
        t_col = sb("t_col", [EDGE_TILE, 2, CHUNK])
        n_match = sb("n_match", [EDGE_TILE, 2, CHUNK])
        to_spare = sb("to_spare", [EDGE_TILE, 2, CHUNK])
        go_spare = sb("go_spare", [EDGE_TILE, 2, CHUNK])
        sums_out = sb("sums_out", [EDGE_TILE, 2, CHUNK, EDGE_DIM])
        rows_out = sb("rows_out", [EDGE_TILE, 2, CHUNK], I32)
        tile_min, tile_max = sb("tile_min", [chunks, CHUNK]), sb("tile_max", [chunks, CHUNK])
        conflict = sb("conflict", [1, tiles], I32)
        tile_no = sb("tile_no", [chunks, CHUNK])
        group_end = sb("group_end", [chunks, groups])
        reach_max = sb("reach_max", [chunks, groups])
        need_col = sb("need_col", [g_half, 2])
        tiles_needed = sb("tiles_needed", [1, groups], I32)

        x_in = sb("x_in", [128, RING, GROUP])
        x_hi, x_lo = sb("x_hi", [128, 2, GROUP], F32R), sb("x_lo", [128, 2, GROUP], F32R)
        agg_in = sb("agg_in", [NODES_P, AGG_RING, NODES_J, EDGE_DIM])
        agg_hl = sb("agg_hl", [NODES_P, 2, NODES_J, 2, EDGE_DIM])
        aggT = sb("aggT", [2 * EDGE_DIM, 2, GROUP], F32R)
        h1, h2 = sb("h1", [128, HALVES, GROUP]), sb("h2", [128, HALVES, GROUP])
        h1_hi, h1_lo = sb("h1_hi", [128, 2, HALVES, GROUP], F32R), sb("h1_lo", [128, 2, HALVES, GROUP], F32R)
        h2_hi, h2_lo = sb("h2_hi", [128, 2, HALVES, GROUP], F32R), sb("h2_lo", [128, 2, HALVES, GROUP], F32R)
        yT = sb("yT", [128, 2, GROUP])
        y_rows = sb("y_rows", [NODES_P, RING, NODES_J, NODE_DIM])
        stats = sb("stats", [NODES_P, RING, NODES_J, 6])
        n_stat = NORM_BATCH * NODES_J
        st = sb("st", [NODES_P, 8, n_stat])
        mean, rstd = sb("mean", [NODES_P, 2, n_stat]), sb("rstd", [NODES_P, 2, n_stat])
        out_rows = sb("out_rows", [128, OUT_RING, NODES_J, NODE_DIM])

        def within(tensor, at, p, shape):
            n = int(np.prod(shape))
            dims = "a b c d"[:2 * len(shape) - 1]
            return tensor[0:p, at:at + n].rearrange(f"q ({dims}) -> q {dims}",
                                                  **dict(zip(dims.split()[1:], shape[1:])))

        y_flat = y_rows[:].rearrange("p g j c -> p (g j c)")
        x_flat = x_in[:].rearrange("p g n -> p (g n)")
        t_row = within(y_flat, 0, EDGE_TILE, (2, CHUNK, EDGE_TILE))
        reach = within(y_flat, 2 * CHUNK * EDGE_TILE, chunks, (CHUNK, groups))
        match = within(h1_hi[:].rearrange("p a b c -> p (a b c)"), 0, EDGE_TILE, (2, CHUNK, EDGE_TILE))
        h1_lo_flat = h1_lo[:].rearrange("p a b c -> p (a b c)")
        edges_hi = within(h1_lo_flat, 0, EDGE_TILE, (2, CHUNK, EDGE_DIM))
        edges_lo = within(h1_lo_flat, 2 * CHUNK * EDGE_DIM, EDGE_TILE, (2, CHUNK, EDGE_DIM))
        select = within(h2_hi[:].rearrange("p a b c -> p (a b c)"), 0, 128, (2, EDGE_TILE))
        h2_lo_flat = h2_lo[:].rearrange("p a b c -> p (a b c)")
        target_parts = within(h2_lo_flat, 0, 128, (CHUNK * EDGE_TILE,))
        targets_hi = within(h2_lo_flat, CHUNK * EDGE_TILE, 128, (CHUNK * EDGE_TILE,))
        min_row, max_row = within(x_flat, 0, 1, (tiles,)), within(x_flat, tiles, 1, (tiles,))
        below, above, overlap = (within(x_flat, (2 + 2 * k) * tiles, 1, (2, tiles)) for k in range(3))
        zeros = out_rows[:].rearrange("p g j c -> p (g j c)")

        bank = [ctx.enter_context(nc.psum_tensor(f"bank{i}", [128, 512], F32)) for i in range(7)]
        l1_ps, l2_ps = bank[0:2], bank[2:4]
        l3_ps, yT_ps, aggT_ps = bank[4], bank[5], bank[6]
        t_row_ps, sums_ps = bank[0:2], bank[2:4]

        ident_made, lower_made, consts_made = sem("ident_made"), sem("lower_made"), sem("consts_made")
        pick_made = sem("pick_made")
        zeros_made, table_zeroed = sem("zeros_made"), sem("table_zeroed")
        targets_landed, by_tile_landed = sem("targets_landed"), sem("by_tile_landed")
        weights_landed, weights_split = sem("weights_landed"), sem("weights_split")
        ranges_done, ranges_rowed, flags_done = sem("ranges_done"), sem("ranges_rowed"), sem("flags_done")
        reach_done, reach_rowed, need_done, need_rowed, needs_ready = (
            sem("reach_done"), sem("reach_rowed"), sem("need_done"), sem("need_rowed"), sem("needs_ready"))
        dve_setup = sem("dve_setup")
        edges_landed = [sem(f"edges_landed{b}") for b in range(2)]
        staged, spread, t_row_ready = sem("staged"), sem("spread"), sem("t_row_ready")
        parts_ready, selected = sem("parts_ready"), sem("selected")
        edges_hi_ready, edges_lo_ready = sem("edges_hi_ready"), sem("edges_lo_ready")
        matched, summed, sums_stored = sem("matched"), sem("summed"), sem("sums_stored")
        spare_chosen, rows_ready, copied_out = sem("spare_chosen"), sem("rows_ready"), sem("copied_out")
        scattered = [sem(f"scattered{u}") for u in range(CHUNK)]
        tiles_landed = sem("tiles_landed")
        x_landed = [sem(f"x_landed{r}") for r in range(RING)]
        agg_landed = [sem(f"agg_landed{r}") for r in range(AGG_RING)]
        out_stored = [sem(f"out_stored{r}") for r in range(OUT_RING)]
        agg_hi_ready, agg_split, aggT_done, aggT_ready = (
            sem("agg_hi_ready"), sem("agg_split"), sem("aggT_done"), sem("aggT_ready"))
        x_hi_ready, x_lo_ready = sem("x_hi_ready"), sem("x_lo_ready")
        l1_done, h1_ready, h1_hi_ready, h1_lo_ready = (
            sem("l1_done"), sem("h1_ready"), sem("h1_hi_ready"), sem("h1_lo_ready"))
        l2_done, h2_ready, h2_hi_ready, h2_lo_ready = (
            sem("l2_done"), sem("h2_ready"), sem("h2_hi_ready"), sem("h2_lo_ready"))
        l3_done, yT_ready, y_turned, y_rows_ready = (
            sem("l3_done"), sem("yT_ready"), sem("y_turned"), sem("y_rows_ready"))
        stats_ready, norm_chain, norm_done = sem("stats_ready"), sem("norm_chain"), sem("norm_done")

        zero_dmas = zeros_n // zero_cols + 1
        assert zero_dmas // 2 < chunks // 2
        front = [Step(0, s, groups) for s in range(-4, 2 * RING)]
        tail = [Step(0, s, groups) for s in range(groups - RING, groups + LAG)]

        def node_steps(eng, step):
            for s in front:
                step(s)
            with eng.Fori(2, groups // RING - 1) as i:
                for off in range(RING):
                    step(Step(i, off, groups))
            for s in tail:
                step(s)

        block = ctx.enter_context(nc.Block())

        @block.sync
        def _(sp):
            for at in (0, LO_ROWS):
                sp.dma_start(targets_by_chunk[at:at + chunks, :, :], target_rows).then_inc(by_tile_landed, 16)
            sp.dma_start(targets[:], target_cols).then_inc(targets_landed, 16)

            def load_edges(c, b):
                sp.dma_start(edges[:, bass.ds(c * CHUNK, CHUNK), :],
                             edge_rows[:, bass.ds(c * CHUNK, CHUNK), :]).then_inc(edges_landed[b], 16)

            flat = table.rearrange("n c -> (n c)")
            node_part = flat[0:nodes * EDGE_DIM].rearrange("(p z) -> p z", p=128)

            def zero_table(k):
                sp.dma_start(node_part[:, bass.ds(k * zero_cols, zero_cols)], zeros[:, 0:zero_cols])\
                    .then_inc(table_zeroed, 16)

            load_edges(0, 0)
            load_edges(1, 1)
            for dst, src in ((w1x_raw[:], W1[0:NODE_DIM, :]),
                             (w1e_raw[0:EDGE_DIM, :], W1[NODE_DIM:, :]),
                             (w1e_raw[EDGE_DIM:, :], W1[NODE_DIM:, :]),
                             (w2_raw[:], W2.rearrange("(t p) n -> p t n", p=128)),
                             (w3_raw[:], W3.rearrange("(t p) n -> p t n", p=128)),
                             (b1_col[:], b1), (b2_col[:], b2), (b3_col[:], b3)):
                sp.dma_start(dst, src).then_inc(weights_landed, 16)
            sp.wait_ge(zeros_made, 1)
            n = spare_rows * EDGE_DIM // 128
            sp.dma_start(flat[nodes * EDGE_DIM:].rearrange("(p z) -> p z", z=n), zeros[:, 0:n])\
                .then_inc(table_zeroed, 16)

            def load_pair(i, zero):
                for b in range(2):
                    sp.wait_ge(edges_landed[b], 16 * i)
                    load_edges(2 * i + b, b)
                if zero:
                    for k in range(2):
                        zero_table(2 * i - 2 + k)

            pairs = (zero_dmas - 1) // 2
            with sp.Fori(1, pairs + 1) as i:
                load_pair(i, True)
            if pairs + 1 < chunks // 2:
                with sp.Fori(pairs + 1, chunks // 2) as i:
                    load_pair(i, False)

            sp.wait_ge(needs_ready, 1)

            def step(s):
                if s.has(3):
                    if s.has(3 - RING):
                        sp.wait_ge(yT_ready, s.done(3 - RING))
                    sp.dma_start(x_in[:, s.slot(3), :],
                                 xT[bass.ds(s.group(3), 1), :, :].rearrange("g p n -> p (g n)"))\
                        .then_inc(x_landed[s.slot(3)], 16)
                if s.has(4):
                    if s.has(4 - AGG_RING):
                        sp.wait_ge(agg_split, s.done(4 - AGG_RING))
                    need = sp.value_load(tiles_needed[0:1, bass.ds(s.group(4), 1)], min_val=1, max_val=tiles)
                    sp.wait_ge(tiles_landed, need)
                    sp.dma_start(agg_in[:, s.slot(4, AGG_RING), :, :].rearrange("p j c -> p (j c)"),
                                 table[bass.ds(s.group(4) * GROUP, GROUP), :]
                                 .rearrange("(p j) c -> p (j c)", j=NODES_J))\
                        .then_inc(agg_landed[s.slot(4, AGG_RING)], 16)
                if s.has(-LAG):
                    sp.wait_ge(norm_done, s.done(-LAG))
                    sp.dma_start(out[bass.ds(s.group(-LAG) * GROUP, GROUP), :]
                                 .rearrange("(p j) c -> p (j c)", j=NODES_J),
                                 out_rows[0:NODES_P, s.slot(-LAG, OUT_RING), :, :].rearrange("p j c -> p (j c)"))\
                        .then_inc(out_stored[s.slot(-LAG, OUT_RING)], 16)

            node_steps(sp, step)
            for r in range(OUT_RING):
                sp.wait_ge(out_stored[r], 16 * (groups // OUT_RING))

        @block.gpsimd
        def _(pool):
            nc.gpsimd.memset(ident[:], 0.0).then_inc(ident_made, 1)
            nc.gpsimd.memset(lower[:], 1.0).then_inc(lower_made, 1)
            pool.wait_ge(ident_made, 1)
            nc.gpsimd.affine_select(out=ident[:], in_=ident[:], compare_op=ALU.not_equal, fill=1.0, base=0,
                                    pattern=[[-1, 128]], channel_multiplier=1).then_inc(ident_made, 1)
            pool.wait_ge(lower_made, 1)
            nc.gpsimd.affine_select(out=lower[:], in_=lower[:], compare_op=ALU.is_ge, fill=0.0, base=0,
                                    pattern=[[-1, EDGE_TILE]], channel_multiplier=1).then_inc(lower_made, 1)
            nc.gpsimd.iota(spare[:], [[EDGE_TILE, CHUNK]], base=nodes, channel_multiplier=1,
                           allow_small_or_imprecise_dtypes=True).then_inc(consts_made, 1)
            nc.gpsimd.memset(pick[:], 0.0).then_inc(pick_made, 1)
            pool.wait_ge(pick_made, 1)
            nc.gpsimd.affine_select(out=pick[:], in_=pick[:], compare_op=ALU.not_equal, fill=1.0, base=0,
                                    pattern=[[-1, chunks]], channel_multiplier=1).then_inc(pick_made, 1)
            pool.wait_ge(pick_made, 2)
            nc.gpsimd.affine_select(out=pick[:], in_=pick[:], compare_op=ALU.not_equal, fill=1.0, base=-LO_ROWS,
                                    pattern=[[-1, chunks]], channel_multiplier=1).then_inc(pick_made, 1)
            nc.gpsimd.iota(tile_no[:], [[1, CHUNK]], base=1, channel_multiplier=CHUNK,
                           allow_small_or_imprecise_dtypes=True).then_inc(consts_made, 1)
            nc.gpsimd.iota(group_end[:], [[GROUP, groups]], base=GROUP, channel_multiplier=0,
                           allow_small_or_imprecise_dtypes=True).then_inc(consts_made, 1)

            pool.wait_ge(flags_done, 1)
            pool.wait_ge(table_zeroed, 16 * zero_dmas)

            def landed(c, u, back):
                v = u - back
                pool.wait_ge(scattered[v % CHUNK], 16 * (c + v // CHUNK + 1))

            def scatter_chunk(c, b, first=False):
                pool.wait_ge(sums_stored, c + 1)
                nc.gpsimd.tensor_copy(sums_out[:, b, :, :].rearrange("p u c -> p (u c)"),
                                      edges[:, bass.ds(c * CHUNK, CHUNK), :].rearrange("p u c -> p (u c)"))\
                    .then_inc(copied_out, 1)
                pool.wait_ge(rows_ready, c + 1)
                nc.gpsimd.tensor_copy(rows_out[:, b, :], scatter_rows[:, bass.ds(c * CHUNK, CHUNK)])\
                    .then_inc(copied_out, 1)
                pool.wait_ge(copied_out, 2 * c + 2)
                for u in range(CHUNK):
                    if not first or u >= IN_FLIGHT:
                        landed(c, u, IN_FLIGHT)
                        pool.sem_inc(tiles_landed, 1)
                    if not first or u > 0:
                        flag = pool.value_load(conflict[0:1, bass.ds(c * CHUNK + u, 1)], min_val=0, max_val=1)
                        with pool.If(flag > 0):
                            for back in range(1, IN_FLIGHT):
                                if not first or u >= back:
                                    landed(c, u, back)
                    nc.gpsimd.indirect_dma_start(
                        table, bass.IndirectOffsetOnAxis(ap=rows_out[:, b, u:u + 1], axis=0),
                        sums_out[:, b, u, :], None, bounds_check=nodes + spare_rows - 1, oob_is_err=True,
                        compute_op=ALU.add).then_inc(scattered[u], 16)

            scatter_chunk(0, 0, first=True)
            scatter_chunk(1, 1)
            with pool.Fori(1, chunks // 2) as i:
                for b in range(2):
                    scatter_chunk(2 * i + b, b)
            for u in range(IN_FLIGHT):
                landed(chunks, u, IN_FLIGHT)
                pool.sem_inc(tiles_landed, 1)

        @block.tensor
        def _(pe):
            pe.wait_ge(ident_made, 2)

            pe.wait_ge(ranges_done, 2)
            for u in range(CHUNK):
                nc.tensor.matmul(bank[4][0:1, u * chunks:(u + 1) * chunks], tile_min[:, u:u + 1],
                                 ident[0:chunks, 0:chunks], start=True, stop=True)
                last = nc.tensor.matmul(bank[5][0:1, u * chunks:(u + 1) * chunks], tile_max[:, u:u + 1],
                                        ident[0:chunks, 0:chunks], start=True, stop=True)
            last.then_inc(ranges_rowed, 1)

            def spread_targets(c, b):
                pe.wait_ge(selected, c + 1)
                for n in range(2):
                    if not isinstance(c, int) or c > 0:
                        pe.wait_ge(t_row_ready, 2 * c + n - 1)
                    half = slice(n * 4 * EDGE_TILE, (n + 1) * 4 * EDGE_TILE)
                    nc.tensor.matmul(t_row_ps[n][0:EDGE_TILE, 0:4 * EDGE_TILE], select[:, b, :],
                                     target_parts[:, half], start=True, stop=True).then_inc(spread, 1)

            def sum_chunk(c, b):
                pe.wait_ge(edges_lo_ready, c + 1)
                if not isinstance(c, int) or c > 1:
                    pe.wait_ge(sums_stored, c - 1)
                for u in range(CHUNK):
                    pe.wait_ge(matched, c * CHUNK + u + 1)
                    o = sums_ps[b][0:EDGE_TILE, u * EDGE_DIM:(u + 1) * EDGE_DIM]
                    nc.tensor.matmul(o, match[:, b, u, :], edges_hi[:, b, u, :], start=True, stop=False)
                    last = nc.tensor.matmul(o, match[:, b, u, :], edges_lo[:, b, u, :], start=False, stop=True)
                last.then_inc(summed, 1)

            pe.wait_ge(parts_ready, 1)
            spread_targets(0, 0)
            spread_targets(1, 1)
            sum_chunk(0, 0)
            spread_targets(2, 0)
            sum_chunk(1, 1)
            with pe.Fori(1, chunks // 2 - 1) as i:
                spread_targets(2 * i + 1, 1)
                sum_chunk(2 * i, 0)
                spread_targets(2 * i + 2, 0)
                sum_chunk(2 * i + 1, 1)
            spread_targets(chunks - 1, 1)
            sum_chunk(chunks - 2, 0)
            sum_chunk(chunks - 1, 1)

            pe.wait_ge(reach_done, 1)
            for h in range(2):
                last = nc.tensor.matmul(bank[4 + h][0:g_half, 0:chunks], reach_max[:, h * g_half:(h + 1) * g_half],
                                        ident[0:chunks, 0:chunks], start=True, stop=True)
            last.then_inc(reach_rowed, 1)
            pe.wait_ge(need_done, 2)
            for h in range(2):
                last = nc.tensor.matmul(bank[6][0:1, h * g_half:(h + 1) * g_half], need_col[:, h:h + 1],
                                        ident[0:g_half, 0:g_half], start=True, stop=True)
            last.then_inc(need_rowed, 1)

            pe.wait_ge(weights_split, 1)
            pe.wait_ge(t_row_ready, 2 * chunks)
            pe.wait_ge(sums_stored, chunks)
            pe.wait_ge(needs_ready, 1)

            def step(s):
                if s.has(0):
                    d = s.off % 2
                    pe.wait_ge(x_lo_ready, s.done(0))
                    pe.wait_ge(aggT_ready, s.done(0))
                    for m in range(HALVES):
                        cols = slice(m * 128, (m + 1) * 128)
                        if s.has(-1):
                            pe.wait_ge(h1_ready, s.done(-1, per=2, plus=m + 1))
                        o = l1_ps[m][:, 0:GROUP]
                        nc.tensor.matmul(o, w1x_hi[:, cols], x_hi[:, d, :], start=True, stop=False)
                        nc.tensor.matmul(o, w1x_hi[:, cols], x_lo[:, d, :], start=False, stop=False)
                        nc.tensor.matmul(o, w1x_lo[:, cols], x_hi[:, d, :], start=False, stop=False)
                        nc.tensor.matmul(o, w1e_hi[:, cols], aggT[:, d, :], start=False, stop=False)
                        nc.tensor.matmul(o, w1e_lo[:, cols], aggT[:, d, :], start=False, stop=True)\
                            .then_inc(l1_done, 1)
                if s.has(1):
                    d = (s.off + 1) % 2
                    pe.wait_ge(agg_split, s.done(1))
                    if s.has(0):
                        pe.wait_ge(aggT_ready, s.done(0))
                    for j in range(NODES_J):
                        last = nc.tensor.transpose(
                            aggT_ps[0:2 * EDGE_DIM, j * NODES_P:(j + 1) * NODES_P],
                            agg_hl[:, d, j, :, :].rearrange("p h c -> p (h c)"),
                            ident[0:NODES_P, 0:NODES_P])
                    last.then_inc(aggT_done, 1)
                if s.has(-2):
                    d = s.off % 2
                    o = l3_ps[:, 0:GROUP]
                    if s.has(-3):
                        pe.wait_ge(yT_ready, s.done(-3))
                    for t in range(HALVES):
                        pe.wait_ge(h2_lo_ready, s.done(-2, per=2, plus=t + 1))
                        nc.tensor.matmul(o, w3_hi[:, t, :], h2_hi[:, d, t, :], start=(t == 0), stop=False)
                        nc.tensor.matmul(o, w3_hi[:, t, :], h2_lo[:, d, t, :], start=False, stop=False)
                        last = nc.tensor.matmul(o, w3_lo[:, t, :], h2_hi[:, d, t, :], start=False,
                                                stop=(t == HALVES - 1))
                    last.then_inc(l3_done, 1)
                if s.has(-1):
                    d = (s.off - 1) % 2
                    pe.wait_ge(h1_lo_ready, s.done(-1))
                    for m in range(HALVES):
                        cols = slice(m * 128, (m + 1) * 128)
                        if s.has(-2):
                            pe.wait_ge(h2_ready, s.done(-2, per=2, plus=m + 1))
                        o = l2_ps[m][:, 0:GROUP]
                        for t in range(HALVES):
                            nc.tensor.matmul(o, w2_hi[:, t, cols], h1_hi[:, d, t, :], start=(t == 0), stop=False)
                            nc.tensor.matmul(o, w2_hi[:, t, cols], h1_lo[:, d, t, :], start=False, stop=False)
                            last = nc.tensor.matmul(o, w2_lo[:, t, cols], h1_hi[:, d, t, :], start=False,
                                                    stop=(t == HALVES - 1))
                        last.then_inc(l2_done, 1)
                if s.has(-3):
                    d = (s.off - 3) % 2
                    pe.wait_ge(yT_ready, s.done(-3))
                    if s.has(-4):
                        pe.wait_ge(y_rows_ready, s.done(-4))
                    for j in range(NODES_J):
                        last = nc.tensor.transpose(yT_ps[0:NODES_P, j * NODE_DIM:(j + 1) * NODE_DIM],
                                                   yT[:, d, j * NODES_P:(j + 1) * NODES_P], ident[:])
                    last.then_inc(y_turned, 1)

            node_steps(pe, step)

        @block.scalar
        def _(act):
            def copy_targets(c, b):
                for n in range(2):
                    act.wait_ge(spread, 2 * c + n + 1)
                    if not isinstance(c, int) or c > 1:
                        act.wait_ge(matched, (c - 2) * CHUNK + 4 * n + 4)
                    nc.scalar.activation(
                        t_row[:, b, 4 * n:4 * n + 4, :].rearrange("p u e -> p (u e)"),
                        t_row_ps[n][0:EDGE_TILE, 0:4 * EDGE_TILE], ACT.Copy).then_inc(t_row_ready, 1)

            def split_edges(c, b):
                act.wait_ge(edges_landed[b], 16 * (c // 2 + 1) if isinstance(c, int) else 8 * (c - b) + 16)
                if not isinstance(c, int) or c > 1:
                    act.wait_ge(summed, c - 1)
                nc.scalar.activation(edges_hi[:, b, :, :].rearrange("p u c -> p (u c)"),
                                     edges[:, bass.ds(c * CHUNK, CHUNK), :].rearrange("p u c -> p (u c)"),
                                     ACT.Copy).then_inc(edges_hi_ready, 1)

            def store_sums(c, b):
                act.wait_ge(summed, c + 1)
                nc.scalar.activation(
                    edges[:].rearrange("p (c u) e -> p c (u e)", u=CHUNK)[:, bass.ds(c, 1), :]
                    .rearrange("p o e -> p (o e)"),
                    sums_ps[b][0:EDGE_TILE, 0:CHUNK * EDGE_DIM], ACT.Copy).then_inc(sums_stored, 1)

            split_edges(0, 0)
            copy_targets(0, 0)
            split_edges(1, 1)
            copy_targets(1, 1)
            store_sums(0, 0)
            split_edges(2, 0)
            copy_targets(2, 0)
            store_sums(1, 1)
            with act.Fori(1, chunks // 2 - 1) as i:
                split_edges(2 * i + 1, 1)
                copy_targets(2 * i + 1, 1)
                store_sums(2 * i, 0)
                split_edges(2 * i + 2, 0)
                copy_targets(2 * i + 2, 0)
                store_sums(2 * i + 1, 1)
            split_edges(chunks - 1, 1)
            copy_targets(chunks - 1, 1)
            store_sums(chunks - 2, 0)
            store_sums(chunks - 1, 1)

            act.wait_ge(weights_landed, 16 * 8)

            def step(s):
                if s.has(1):
                    d = (s.off + 1) % 2
                    act.wait_ge(x_landed[s.slot(1)], s.landed(1))
                    if s.has(-1):
                        act.wait_ge(l1_done, s.done(-1, per=2))
                    nc.scalar.activation(x_hi[:, d, :], x_in[:, s.slot(1), :], ACT.Copy).then_inc(x_hi_ready, 1)
                if s.has(0):
                    d = s.off % 2
                    if s.has(-1):
                        act.wait_ge(h1_lo_ready, s.done(-1))
                    for m in range(HALVES):
                        act.wait_ge(l1_done, s.done(0, per=2, plus=m + 1))
                        nc.scalar.activation(h1[:, m, :], l1_ps[m][:, 0:GROUP], ACT.Silu,
                                             bias=b1_col[:, m:m + 1]).then_inc(h1_ready, 1)
                if s.has(1):
                    d = (s.off + 1) % 2
                    act.wait_ge(aggT_done, s.done(1))
                    nc.scalar.activation(aggT[:, d, :], aggT_ps[0:2 * EDGE_DIM, 0:GROUP], ACT.Copy)\
                        .then_inc(aggT_ready, 1)
                if s.has(0):
                    d = s.off % 2
                    act.wait_ge(h1_ready, s.done(0, per=2))
                    if s.has(-2):
                        act.wait_ge(l2_done, s.done(-2, per=2))
                    nc.scalar.activation(h1_hi[:, d, :, :].rearrange("p t n -> p (t n)"),
                                         h1[:].rearrange("p t n -> p (t n)"), ACT.Copy)\
                        .then_inc(h1_hi_ready, 1)
                if s.has(-1):
                    d = (s.off - 1) % 2
                    if s.has(-2):
                        act.wait_ge(h2_lo_ready, s.done(-2, per=2))
                    for m in range(HALVES):
                        act.wait_ge(l2_done, s.done(-1, per=2, plus=m + 1))
                        nc.scalar.activation(h2[:, m, :], l2_ps[m][:, 0:GROUP], ACT.Silu,
                                             bias=b2_col[:, m:m + 1]).then_inc(h2_ready, 1)
                        act.wait_ge(h2_ready, s.done(-1, per=2, plus=m + 1))
                        if s.has(-3):
                            act.wait_ge(l3_done, s.done(-3))
                        nc.scalar.activation(h2_hi[:, d, m, :], h2[:, m, :], ACT.Copy).then_inc(h2_hi_ready, 1)
                if s.has(-3):
                    act.wait_ge(y_turned, s.done(-3))
                    if s.has(-3 - RING):
                        act.wait_ge(norm_done, s.done(-3 - RING))
                    nc.scalar.activation(y_rows[:, s.slot(-3), :, :].rearrange("p j c -> p (j c)"),
                                         yT_ps[0:NODES_P, :], ACT.Copy).then_inc(y_rows_ready, 1)

            node_steps(act, step)

        @block.vector
        def _(dve):
            nc.vector.memset(zeros[:, 0:zero_cols], 0.0).then_inc(zeros_made, 1)

            dve.wait_ge(by_tile_landed, 32)
            nc.vector.tensor_reduce(tile_min[:], targets_by_chunk[0:chunks, :, :], AX_X, ALU.min)\
                .then_inc(ranges_done, 1)
            nc.vector.tensor_reduce(tile_max[:], targets_by_chunk[0:chunks, :, :], AX_X, ALU.max)\
                .then_inc(ranges_done, 1)
            nc.vector.memset(target_parts.bitcast(F32), 0.0).then_inc(dve_setup, 1)
            top, bottom = slice(0, chunks), slice(LO_ROWS, LO_ROWS + chunks)
            raw = targets_by_chunk[:].rearrange("p u e -> p (u e)")
            nc.vector.tensor_copy(targets_hi[bottom, :], raw[bottom, :]).then_inc(dve_setup, 1)
            dve.wait_ge(dve_setup, 2)
            nc.vector.tensor_copy(target_parts[top, :], raw[top, :])
            nc.vector.tensor_tensor(target_parts[bottom, :], raw[bottom, :], targets_hi[bottom, :].bitcast(F32),
                                    ALU.subtract).then_inc(parts_ready, 1)

            def stage(c, b):
                if not isinstance(c, int) or c > 1:
                    dve.wait_ge(spare_chosen, 2 * c - 3)
                nc.vector.tensor_copy(t_col[:, b, :], targets[:, bass.ds(c * CHUNK, CHUNK)]).then_inc(staged, 1)
                if not isinstance(c, int) or c > 1:
                    dve.wait_ge(spread, 2 * c - 2)
                nc.vector.tensor_copy(select[:, b, :], pick[:, bass.ds(c, 1)].to_broadcast([128, EDGE_TILE]))\
                    .then_inc(selected, 1)

            def edges_low(c, b):
                dve.wait_ge(edges_hi_ready, c + 1)
                nc.vector.tensor_tensor(edges_lo[:, b, :, :].rearrange("p u c -> p (u c)"),
                                        edges[:, bass.ds(c * CHUNK, CHUNK), :].rearrange("p u c -> p (u c)"),
                                        edges_hi[:, b, :, :].rearrange("p u c -> p (u c)").bitcast(F32),
                                        ALU.subtract).then_inc(edges_lo_ready, 1)

            dve.wait_ge(targets_landed, 16)
            dve.wait_ge(pick_made, 3)
            stage(0, 0)

            dve.wait_ge(ranges_rowed, 1)
            nc.vector.tensor_copy(min_row.rearrange("o (c u) -> o c u", u=CHUNK),
                                  bank[4][0:1, 0:tiles].rearrange("o (u c) -> o c u", u=CHUNK)).then_inc(dve_setup, 1)
            nc.vector.tensor_copy(max_row.rearrange("o (c u) -> o c u", u=CHUNK),
                                  bank[5][0:1, 0:tiles].rearrange("o (u c) -> o c u", u=CHUNK)).then_inc(dve_setup, 1)
            nc.vector.memset(overlap[:], 0.0).then_inc(dve_setup, 1)
            dve.wait_ge(dve_setup, 5)
            for n in range(2):
                back = n + 1
                nc.vector.tensor_tensor(below[:, n, back:], min_row[:, back:], max_row[:, :tiles - back], ALU.is_le)\
                    .then_inc(dve_setup, 1)
                nc.vector.tensor_tensor(above[:, n, back:], max_row[:, back:], min_row[:, :tiles - back], ALU.is_ge)\
                    .then_inc(dve_setup, 1)
            dve.wait_ge(dve_setup, 9)
            for n in range(2):
                back = n + 1
                nc.vector.tensor_tensor(overlap[:, n, back:], below[:, n, back:], above[:, n, back:], ALU.mult)\
                    .then_inc(dve_setup, 1)
            dve.wait_ge(dve_setup, 11)
            nc.vector.tensor_tensor(conflict[:], overlap[:, 0, :], overlap[:, 1, :], ALU.max).then_inc(flags_done, 1)

            dve.wait_ge(lower_made, 2)
            dve.wait_ge(consts_made, 3)

            def match_tile(c, b, u):
                nc.vector.scalar_tensor_tensor(match[:, b, u, :], t_row[:, b, u, :], t_col[:, b, u:u + 1],
                                               lower[:], ALU.is_equal, ALU.mult,
                                               accum_out=n_match[:, b, u:u + 1]).then_inc(matched, 1)

            def choose_spare(c, b):
                dve.wait_ge(matched, (c + 1) * CHUNK)
                dve.wait_ge(spare_chosen, 2 * c + 1)
                nc.vector.scalar_tensor_tensor(go_spare[:, b, :], n_match[:, b, :], 1.5, to_spare[:, b, :],
                                               ALU.is_gt, ALU.mult).then_inc(spare_chosen, 1)

            def choose_rows(c, b):
                dve.wait_ge(spare_chosen, 2 * c + 2)
                nc.vector.tensor_tensor(scatter_rows[:, bass.ds(c * CHUNK, CHUNK)], go_spare[:, b, :],
                                        targets[:, bass.ds(c * CHUNK, CHUNK)], ALU.add).then_inc(rows_ready, 1)

            def match_chunk(c, b, first=False, last=False):
                if not last:
                    stage(c + 1, 1 - b)
                    edges_low(c + 1, 1 - b)
                if not isinstance(c, int) or c > 1:
                    dve.wait_ge(summed, c - 1)
                dve.wait_ge(staged, c + 1)
                for u in range(CHUNK):
                    if u % 4 == 0:
                        dve.wait_ge(t_row_ready, 2 * c + u // 4 + 1)
                    match_tile(c, b, u)
                    if u == 1 and not first:
                        choose_spare(c - 1, 1 - b)
                    if u == 4 and not first:
                        choose_rows(c - 1, 1 - b)
                nc.vector.tensor_tensor(to_spare[:, b, :], spare[:], t_col[:, b, :], ALU.subtract)\
                    .then_inc(spare_chosen, 1)

            edges_low(0, 0)
            match_chunk(0, 0, first=True)
            match_chunk(1, 1)
            with dve.Fori(1, chunks // 2 - 1) as i:
                match_chunk(2 * i, 0)
                match_chunk(2 * i + 1, 1)
            match_chunk(chunks - 2, 0)
            match_chunk(chunks - 1, 1, last=True)
            choose_spare(chunks - 1, 1)
            choose_rows(chunks - 1, 1)

            for u in range(CHUNK):
                nc.vector.tensor_scalar(reach[:, u, :], group_end[:], tile_min[:, u:u + 1], tile_no[:, u:u + 1],
                                        ALU.is_gt, ALU.mult).then_inc(dve_setup, 1)
            dve.wait_ge(dve_setup, 11 + CHUNK)
            nc.vector.tensor_reduce(reach_max[:], reach.rearrange("p u g -> p g u"), AX_X, ALU.max)\
                .then_inc(reach_done, 1)

            dve.wait_ge(weights_landed, 16 * 8)
            nc.vector.tensor_scalar(w3_raw[:], w3_raw[:], 0.5, None, ALU.mult).then_inc(dve_setup, 1)
            nc.vector.tensor_scalar(b3_half[:], b3_col[:], 0.5, None, ALU.mult).then_inc(dve_setup, 1)
            dve.wait_ge(dve_setup, 13 + CHUNK)
            parts = ((w1x_raw, w1x_hi, w1x_lo), (w1e_raw, w1e_hi, w1e_lo), (w2_raw, w2_hi, w2_lo),
                     (w3_raw, w3_hi, w3_lo))
            for raw, hi, lo in parts:
                nc.vector.tensor_copy(hi[:], raw[:]).then_inc(dve_setup, 1)
            dve.wait_ge(dve_setup, 17 + CHUNK)
            for raw, hi, lo in parts:
                last = nc.vector.tensor_tensor(lo[:], raw[:], hi[:].bitcast(F32), ALU.subtract)
            last.then_inc(weights_split, 1)

            dve.wait_ge(reach_rowed, 1)
            for h in range(2):
                nc.vector.tensor_reduce(need_col[:, h:h + 1], bank[4 + h][0:g_half, 0:chunks], AX_X, ALU.max)\
                    .then_inc(need_done, 1)
            dve.wait_ge(need_rowed, 1)
            nc.vector.tensor_scalar(tiles_needed[:], bank[6][0:1, 0:groups], 1.0, None, ALU.max)\
                .then_inc(needs_ready, 1)

            NORM_OPS = 18
            tt, stt, ts = nc.vector.tensor_tensor, nc.vector.scalar_tensor_tensor, nc.vector.tensor_scalar
            tmp = [st[:, k, :] for k in range(8)]

            def norm_op(s, lag, k):
                first = s.slot(-lag)
                q = first // NORM_BATCH
                view = stats[:, first:first + NORM_BATCH, :, :].rearrange("p g j f -> p (g j) f")
                before = (s.ring_no * (RING // NORM_BATCH) + (s.off - lag) // NORM_BATCH) * NORM_OPS
                if k not in (0, 1, 2, 4):
                    dve.wait_ge(norm_chain, before + k)
                if k == 0:
                    ins = tt(tmp[0], view[:, :, 1], view[:, :, 4], ALU.add)
                elif k == 1:
                    ins = tt(tmp[1], view[:, :, 1], view[:, :, 4], ALU.subtract)
                elif k == 2:
                    ins = tt(tmp[2], view[:, :, 2], view[:, :, 5], ALU.add)
                elif k == 3:
                    ins = tt(tmp[3], tmp[1], tmp[1], ALU.mult)
                elif k == 4:
                    dve.wait_ge(norm_chain, before + 1)
                    ins = ts(mean[:, q, :], tmp[0], 0.5, None, ALU.mult)
                elif k == 5:
                    ins = stt(tmp[4], tmp[3], NODE_DIM / 4.0, tmp[2], ALU.mult, ALU.add)
                elif k == 6:
                    ins = ts(tmp[5], tmp[4], 1.0 / NODE_DIM, EPS / 4.0, ALU.mult, ALU.add)
                elif k == 7:
                    ins = ts(tmp[6].bitcast(I32), tmp[5].bitcast(I32), 1, None, ALU.logical_shift_right)
                elif k == 8:
                    ins = ts(tmp[7].bitcast(I32), tmp[6].bitcast(I32), -1.0, float(0x5F3759DF), ALU.mult, ALU.add)
                else:
                    turn, part = divmod(k - 9, 3)
                    y, other = (tmp[7], tmp[6]) if turn % 2 == 0 else (tmp[6], tmp[7])
                    if part == 0:
                        ins = tt(tmp[3], y, y, ALU.mult)
                    elif part == 1:
                        ins = stt(tmp[4], tmp[3], -0.5, tmp[5], ALU.mult, ALU.mult)
                    else:
                        ins = stt(rstd[:, q, :] if turn == 2 else other, tmp[4], 1.5, y, ALU.add, ALU.mult)
                ins.then_inc(norm_chain, 1)

            def step(s):
                first_half = s.off % NORM_BATCH == NORM_BATCH - 1 and s.has(-4)
                second_half = s.off % NORM_BATCH == 0 and s.has(-5)

                def norm_part(k1, k2):
                    if first_half and k1 is not None:
                        norm_op(s, 7, k1)
                    if second_half and k2 is not None:
                        norm_op(s, 8, 9 + k2)

                if s.has(-4):
                    dve.wait_ge(y_rows_ready, s.done(-4))
                    for j in range(NODES_J):
                        last = nc.vector.bn_stats(stats[:, s.slot(-4), j, :], y_rows[:, s.slot(-4), j, :])
                        norm_part(None, j)
                    last.then_inc(stats_ready, 1)
                elif second_half:
                    for k in range(NODES_J):
                        norm_part(None, k)
                if s.has(2):
                    d = s.off % 2
                    dve.wait_ge(agg_landed[s.slot(2, AGG_RING)], s.landed(2, AGG_RING))
                    if s.has(0):
                        dve.wait_ge(aggT_done, s.done(0))
                    nc.vector.tensor_copy(agg_hl[:, d, :, 0, :].bitcast(F32R), agg_in[:, s.slot(2, AGG_RING), :, :])\
                        .then_inc(agg_hi_ready, 1)
                if first_half:
                    dve.wait_ge(stats_ready, s.done(-4))
                norm_part(0, None)
                if s.has(-LAG):
                    q = s.slot(-LAG) // NORM_BATCH
                    if s.has(-LAG - OUT_RING):
                        dve.wait_ge(out_stored[s.slot(-LAG, OUT_RING)], s.landed(-LAG - OUT_RING, OUT_RING))
                    if s.slot(-LAG, NORM_BATCH) == 0:
                        dve.wait_ge(norm_chain, (s.ring_no * (RING // NORM_BATCH) + (s.off - LAG) // NORM_BATCH + 1)
                                    * NORM_OPS)
                    for j in range(NODES_J):
                        k = s.slot(-LAG, NORM_BATCH) * NODES_J + j
                        last = nc.vector.tensor_scalar(out_rows[0:NODES_P, s.slot(-LAG, OUT_RING), j, :],
                                                       y_rows[:, s.slot(-LAG), j, :],
                                                       mean[:, q, k:k + 1], rstd[:, q, k:k + 1],
                                                       ALU.subtract, ALU.mult)
                        if j < NODES_J - 1:
                            norm_part(1 + j, 4 + j)
                    last.then_inc(norm_done, 1)
                else:
                    for k in range(NODES_J - 1):
                        norm_part(1 + k, 4 + k)
                norm_part(4, 7)
                if s.has(2):
                    dve.wait_ge(agg_hi_ready, s.done(2))
                    nc.vector.tensor_tensor(agg_hl[:, d, :, 1, :], agg_in[:, s.slot(2, AGG_RING), :, :],
                                            agg_hl[:, d, :, 0, :], ALU.subtract).then_inc(agg_split, 1)
                norm_part(5, 8)
                if s.has(1):
                    d = (s.off + 1) % 2
                    dve.wait_ge(x_hi_ready, s.done(1))
                    nc.vector.tensor_tensor(x_lo[:, d, :], x_in[:, s.slot(1), :], x_hi[:, d, :].bitcast(F32),
                                            ALU.subtract).then_inc(x_lo_ready, 1)
                norm_part(6, None)
                if s.has(0):
                    d = s.off % 2
                    dve.wait_ge(h1_hi_ready, s.done(0))
                    nc.vector.tensor_tensor(h1_lo[:, d, :, :].rearrange("p t n -> p (t n)"),
                                            h1[:].rearrange("p t n -> p (t n)"),
                                            h1_hi[:, d, :, :].rearrange("p t n -> p (t n)").bitcast(F32),
                                            ALU.subtract).then_inc(h1_lo_ready, 1)
                norm_part(7, None)
                if s.has(-2):
                    d = s.off % 2
                    dve.wait_ge(l3_done, s.done(-2))
                    if s.has(-4):
                        dve.wait_ge(y_turned, s.done(-4))
                    nc.vector.scalar_tensor_tensor(yT[:, d, :], l3_ps[:, 0:GROUP], b3_half[:],
                                                   x_in[:, s.slot(-2), :], ALU.add, ALU.add)\
                        .then_inc(yT_ready, 1)
                norm_part(8, None)
                if s.has(-1):
                    d = (s.off - 1) % 2
                    if s.has(-3):
                        dve.wait_ge(l3_done, s.done(-3))
                    for m in range(HALVES):
                        dve.wait_ge(h2_hi_ready, s.done(-1, per=2, plus=m + 1))
                        nc.vector.tensor_tensor(h2_lo[:, d, m, :], h2[:, m, :], h2_hi[:, d, m, :].bitcast(F32),
                                                ALU.subtract).then_inc(h2_lo_ready, 1)

            node_steps(dve, step)


def kernel(x, src, dst, edge_attr_48, L0_gnn_W1, L0_gnn_b1, L0_gnn_W2, L0_gnn_b2, L0_gnn_W3, L0_gnn_b3):
    import concourse.bacc as bacc
    from concourse.bass_utils import run_bass_kernel_spmd

    x = np.asarray(x)
    nodes = x.shape[0]
    groups = nodes // GROUP
    tiles = np.shape(dst)[0] // EDGE_TILE
    order = np.array([k // CHUNK * CHUNK + k * TILE_STRIDE % CHUNK for k in range(tiles)])
    by_tile = np.asarray(dst).reshape(tiles, EDGE_TILE)[order]
    arrays = {
        "xT": x.reshape(groups, NODES_P, NODES_J, NODE_DIM).transpose(0, 3, 2, 1).reshape(groups, NODE_DIM, GROUP),
        "edge_rows": np.asarray(edge_attr_48).reshape(tiles, EDGE_TILE, EDGE_DIM)[order].transpose(1, 0, 2),
        "target_cols": by_tile.T,
        "target_rows": by_tile.reshape(tiles // CHUNK, CHUNK, EDGE_TILE),
        "W1": np.asarray(L0_gnn_W1),
        "b1": np.asarray(L0_gnn_b1).reshape(HALVES, 128).T,
        "W2": np.asarray(L0_gnn_W2),
        "b2": np.asarray(L0_gnn_b2).reshape(HALVES, 128).T,
        "W3": np.asarray(L0_gnn_W3),
        "b3": np.asarray(L0_gnn_b3).reshape(NODE_DIM, 1),
    }
    arrays = {name: np.ascontiguousarray(a) for name, a in arrays.items()}
    nc = bacc.Bacc("TRN2", target_bir_lowering=False, num_devices=1)
    args = [nc.dram_tensor(name, a.shape, mybir.dt.from_np(a.dtype), kind="ExternalInput").ap()
            for name, a in arrays.items()]
    out = nc.dram_tensor("out", (nodes, NODE_DIM), F32, kind="ExternalOutput").ap()
    build_gnn(nc, *args, out)
    r = run_bass_kernel_spmd(nc, [arrays], core_ids=[0])
    return r.results[0]["out"]
```

```python
from contextlib import ExitStack

import numpy as np

import concourse.bass as bass
from concourse import mybir

F32 = mybir.dt.float32
F32R = mybir.dt.float32r
I32 = mybir.dt.int32
ALU = mybir.AluOpType
ACT = mybir.ActivationFunctionType
AX_X = mybir.AxisListType.X

NODE_DIM = 128
EDGE_DIM = 48
HID = 256
HALVES = HID // 128
NODES_P = 125
NODES_J = 4
GROUP = NODES_P * NODES_J
TURNED = NODES_P + 1
RING = 8
AGG_RING = 4
OUT_RING = 4
LAG = 9
NORM_BATCH = 4
EDGE_TILE = 125
CHUNK = 8
ORDER_BLOCK = 16
TILE_STRIDE = 3
ZERO_PARTS = 30
ZERO_PER_FOUR = 5
CHUNK_PARTS = {2: (0, 1), 3: (2, 3), 4: (), 5: (), 6: (4,), 7: (5,), 8: (6,), 9: (7,), 10: (8,), 11: (9,),
               12: (), 13: (10, 11), 14: (), 15: (12, 13)}
PART_CHUNKS = len(CHUNK_PARTS)
RANGES_CHUNK, REACH_CHUNK, NEED_CHUNK = 4, 11, 13
WARM_UP = 12
LO_ROWS = 64
IN_FLIGHT = 4
EPS = 1e-5


class Step:

    def __init__(self, ring_no, off, groups):
        self.ring_no, self.off, self.groups = ring_no, off, groups
        self.in_loop = not isinstance(ring_no, int)

    def has(self, k):
        return self.in_loop or 0 <= self.ring_no * RING + self.off + k < self.groups

    def done(self, k, per=1, plus=None):
        plus = per if plus is None else plus
        return self.ring_no * (RING * per) + ((self.off + k) * per + plus)

    def slot(self, k, ring=RING):
        return (self.off + k) % ring

    def landed(self, k, ring=RING):
        return self.ring_no * (16 * RING // ring) + 16 * ((self.off + k) // ring + 1)

    def group(self, k):
        return self.ring_no * RING + (self.off + k)

    def first_node(self, k):
        return self.ring_no * (-RING * GROUP) + (self.groups - 1 - self.off - k) * GROUP


def build_gnn(nc, xT, edge_rows, target_cols, target_rows, W1, b1, W2, b2, W3, b3, out):
    groups = xT.shape[0]
    nodes = groups * GROUP
    tiles = edge_rows.shape[1]
    chunks = tiles // CHUNK
    spare_rows = CHUNK * EDGE_TILE
    g_half = groups // 2
    assert edge_rows.shape[0] == EDGE_TILE and tiles % CHUNK == 0 and chunks <= LO_ROWS
    assert groups % RING == 0 and groups >= 4 * RING and g_half <= 128 and chunks % 4 == 2

    with ExitStack() as ctx:
        def sb(name, shape, dt=F32):
            return ctx.enter_context(nc.sbuf_tensor(name, shape, dt))

        def sem(name):
            return ctx.enter_context(nc.semaphore(name))

        table = nc.dram_tensor("node_sums", (nodes + spare_rows, EDGE_DIM), F32, kind="Internal").ap()

        ident = sb("ident", [128, 128])
        ident_r = sb("ident_r", [NODES_P, TURNED], F32R)
        pick = sb("pick", [128, chunks + 1])
        lower = sb("lower", [EDGE_TILE, EDGE_TILE])
        zeros_n = nodes * EDGE_DIM // 128
        zero_cols = zeros_n // (2 * ZERO_PARTS)
        w1x_raw = sb("w1x_raw", [128, HID])
        w1e_raw = sb("w1e_raw", [2 * EDGE_DIM, HID])
        w2_raw = sb("w2_raw", [128, HALVES, HID])
        w3_raw = sb("w3_raw", [128, HALVES, NODE_DIM])
        w1x_hi, w1x_lo = sb("w1x_hi", [128, HID], F32R), sb("w1x_lo", [128, HID], F32R)
        w1e_hi, w1e_lo = sb("w1e_hi", [2 * EDGE_DIM, HID], F32R), sb("w1e_lo", [2 * EDGE_DIM, HID], F32R)
        w2_hi, w2_lo = sb("w2_hi", [128, HALVES, HID], F32R), sb("w2_lo", [128, HALVES, HID], F32R)
        w3_hi, w3_lo = sb("w3_hi", [128, HALVES, NODE_DIM], F32R), sb("w3_lo", [128, HALVES, NODE_DIM], F32R)
        b1_col, b2_col = sb("b1_col", [128, HALVES]), sb("b2_col", [128, HALVES])
        silu_probe = sb("silu_probe", [128, 1])
        b3_col, b3_half = sb("b3_col", [128, 1]), sb("b3_half", [128, 1])

        edges = sb("edges", [EDGE_TILE, tiles, EDGE_DIM])
        targets = sb("targets", [EDGE_TILE, tiles], I32)
        scatter_rows = sb("scatter_rows", [EDGE_TILE, tiles], I32)
        spare = sb("spare", [EDGE_TILE, CHUNK])
        n_match = sb("n_match", [EDGE_TILE, 2, CHUNK])
        go_spare = sb("go_spare", [EDGE_TILE, 2, CHUNK])
        sums_out = sb("sums_out", [EDGE_TILE, 2, CHUNK, EDGE_DIM])
        rows_out = sb("rows_out", [EDGE_TILE, 2, CHUNK], I32)
        tile_min, tile_max = sb("tile_min", [chunks, CHUNK]), sb("tile_max", [chunks, CHUNK])
        conflict = sb("conflict", [1, tiles], I32)
        tile_no = sb("tile_no", [chunks, CHUNK])
        group_start = sb("group_start", [chunks, groups])
        reach_max = sb("reach_max", [chunks, groups])
        need_col = sb("need_col", [g_half, 2])
        tiles_needed = sb("tiles_needed", [1, groups], I32)

        x_in = sb("x_in", [128, RING, GROUP])
        x_hi, x_lo = sb("x_hi", [128, 2, GROUP], F32R), sb("x_lo", [128, 2, GROUP], F32R)
        agg_in = sb("agg_in", [NODES_P, AGG_RING, NODES_J, EDGE_DIM])
        agg_hl = sb("agg_hl", [NODES_P, 2, NODES_J, 2, EDGE_DIM], F32R)
        aggT = sb("aggT", [2 * EDGE_DIM, 2, GROUP], F32R)
        h1, h2 = sb("h1", [128, HALVES, GROUP]), sb("h2", [128, HALVES, GROUP])
        h1_hi, h1_lo = sb("h1_hi", [128, 2, HALVES, GROUP], F32R), sb("h1_lo", [128, 2, HALVES, GROUP], F32R)
        h2_hi, h2_lo = sb("h2_hi", [128, 2, HALVES, GROUP], F32R), sb("h2_lo", [128, 2, HALVES, GROUP], F32R)
        yT = sb("yT", [128, 2, GROUP])
        y_rows = sb("y_rows", [NODES_P, RING, NODES_J, NODE_DIM])
        stats = sb("stats", [NODES_P, RING, NODES_J, 6])
        n_stat = NORM_BATCH * NODES_J
        st = sb("st", [NODES_P, 8, n_stat])
        mean, rstd = sb("mean", [NODES_P, 2, n_stat]), sb("rstd", [NODES_P, 2, n_stat])
        out_rows = sb("out_rows", [128, OUT_RING, NODES_J, NODE_DIM])

        def within(tensor, at, p, shape):
            n = int(np.prod(shape))
            dims = "a b c d"[:2 * len(shape) - 1]
            return tensor[0:p, at:at + n].rearrange(f"q ({dims}) -> q {dims}",
                                                  **dict(zip(dims.split()[1:], shape[1:])))

        y_flat = y_rows[:].rearrange("p g j c -> p (g j c)")
        x_flat = x_in[:].rearrange("p g n -> p (g n)")
        t_row = within(y_flat, 0, EDGE_TILE, (2, CHUNK, EDGE_TILE))
        reach = within(y_flat, 2 * CHUNK * EDGE_TILE, chunks, (CHUNK, groups))
        match = [within(h[:].rearrange("p m n -> p (m n)"), 0, EDGE_TILE, (CHUNK, EDGE_TILE)) for h in (h1, h2)]
        targets_by_chunk = within(yT[:].rearrange("p a n -> p (a n)").bitcast(I32), 0, 128, (CHUNK, EDGE_TILE))
        select = within(h2_hi[:].rearrange("p a b c -> p (a b c)"), 0, 128, (2, EDGE_TILE))
        h2_lo_flat = h2_lo[:].rearrange("p a b c -> p (a b c)")
        target_parts = within(h2_lo_flat, 0, 128, (CHUNK * EDGE_TILE,))
        targets_hi = within(h2_lo_flat, CHUNK * EDGE_TILE, 128, (CHUNK * EDGE_TILE,))
        min_row, max_row = within(x_flat, 0, 1, (tiles,)), within(x_flat, tiles, 1, (tiles,))
        below, above = (within(x_flat, (2 + k * (IN_FLIGHT - 1)) * tiles, 1, (IN_FLIGHT - 1, tiles))
                        for k in range(2))
        assert tiles <= GROUP and 2 * IN_FLIGHT * tiles <= RING * GROUP - 2 * tiles
        t_col = within(x_flat, RING * GROUP - 2 * tiles, EDGE_TILE, (tiles,))
        to_spare = within(x_flat, RING * GROUP - tiles, EDGE_TILE, (tiles,))
        zeros = out_rows[:].rearrange("p g j c -> p (g j c)")

        bank = [ctx.enter_context(nc.psum_tensor(f"bank{i}", [128, 512], F32)) for i in range(8)]
        l1_ps, l2_ps = bank[0:2], bank[2:4]
        l3_ps, yT_ps, aggT_ps = bank[4], bank[5], bank[6]
        t_row_ps, sums_ps = bank[0:4], bank[4:6]

        ident_made, lower_made, consts_made = sem("ident_made"), sem("lower_made"), sem("consts_made")
        pick_made, silu_loaded = sem("pick_made"), sem("silu_loaded")
        parts_cleared, reach_made, flags_done = sem("parts_cleared"), sem("reach_made"), sem("flags_done")
        zeros_made, table_zeroed = sem("zeros_made"), sem("table_zeroed")
        targets_landed, by_chunk_landed = sem("targets_landed"), sem("by_chunk_landed")
        weights_landed, weights_split = sem("weights_landed"), sem("weights_split")
        ranges_rowed = sem("ranges_rowed")
        reach_rowed, need_rowed = sem("reach_rowed"), sem("need_rowed")
        dve_setup, RANGES_DONE, ROWS_DONE, REACH_DONE = sem("dve_setup"), 5, 7, 11
        NEED_DONE, NEEDS_READY, SETUP_DONE = 13, 14, 15
        pool_setup = sem("pool_setup")
        edges_landed = [sem(f"edges_landed{k}") for k in range(4)]
        parts_ready, selected, spread, matched = sem("parts_ready"), sem("selected"), sem("spread"), sem("matched")
        t_row_ready, cols_ready = sem("t_row_ready"), sem("cols_ready")
        summed, sums_stored = sem("summed"), sem("sums_stored")
        spare_chosen, rows_ready, copied_out = sem("spare_chosen"), sem("rows_ready"), sem("copied_out")
        scattered = [sem(f"scattered{u}") for u in range(CHUNK)]
        tiles_landed = sem("tiles_landed")
        x_landed = [sem(f"x_landed{r}") for r in range(RING)]
        agg_landed = [sem(f"agg_landed{r}") for r in range(AGG_RING)]
        out_stored = [sem(f"out_stored{r}") for r in range(OUT_RING)]
        agg_hi_ready, agg_split, aggT_done, aggT_ready = (
            sem("agg_hi_ready"), sem("agg_split"), sem("aggT_done"), sem("aggT_ready"))
        x_hi_ready, x_lo_ready = sem("x_hi_ready"), sem("x_lo_ready")
        l1_done, h1_ready, h1_hi_ready, h1_lo_ready = (
            sem("l1_done"), sem("h1_ready"), sem("h1_hi_ready"), sem("h1_lo_ready"))
        l2_done, h2_ready, h2_hi_ready, h2_lo_ready = (
            sem("l2_done"), sem("h2_ready"), sem("h2_hi_ready"), sem("h2_lo_ready"))
        l3_done, yT_ready, y_turned, y_rows_ready = (
            sem("l3_done"), sem("yT_ready"), sem("y_turned"), sem("y_rows_ready"))
        stats_ready, norm_chain, norm_done = sem("stats_ready"), sem("norm_chain"), sem("norm_done")

        zero_dmas = ZERO_PARTS + 1
        assert zeros_n % (2 * ZERO_PARTS) == 0 and ZERO_PARTS % ZERO_PER_FOUR == 0
        assert zero_cols >= spare_rows * EDGE_DIM // 128
        front = [Step(0, s, groups) for s in range(-4, 2 * RING)]
        tail = [Step(0, s, groups) for s in range(groups - RING, groups + LAG)]

        def node_steps(eng, step):
            for s in front:
                step(s)
            with eng.Fori(2, groups // RING - 1) as i:
                for off in range(RING):
                    step(Step(i, off, groups))
            for s in tail:
                step(s)

        block = ctx.enter_context(nc.Block())

        @block.sync
        def _(sp):
            for at in (0, LO_ROWS):
                sp.dma_start(targets_by_chunk[at:at + chunks, :, :], target_rows).then_inc(by_chunk_landed, 16)
            sp.dma_start(targets[:], target_cols).then_inc(targets_landed, 16)

            def load_edges(c, k):
                sp.dma_start(edges[:, bass.ds(c * CHUNK, CHUNK), :],
                             edge_rows[:, bass.ds(c * CHUNK, CHUNK), :]).then_inc(edges_landed[k], 16)

            flat = table.rearrange("n c -> (n c)")
            node_part = flat[0:nodes * EDGE_DIM].rearrange("(p z) -> p z", p=128)

            def zero_table(k):
                sp.dma_start(node_part[:, bass.ds(k * (2 * zero_cols), 2 * zero_cols)]
                             .rearrange("p (t z) -> p t z", t=2),
                             zeros[:, 0:zero_cols].rearrange("p (o z) -> p o z", o=1)
                             .to_broadcast([128, 2, zero_cols])).then_inc(table_zeroed, 16)

            for c in range(4):
                load_edges(c, c)
            for dst, src in ((w1x_raw[:], W1[0:NODE_DIM, :]),
                             (w1e_raw[0:EDGE_DIM, :], W1[NODE_DIM:, :]),
                             (w1e_raw[EDGE_DIM:, :], W1[NODE_DIM:, :]),
                             (w2_raw[:], W2.rearrange("(t p) n -> p t n", p=128)),
                             (w3_raw[:], W3.rearrange("(t p) n -> p t n", p=128)),
                             (b1_col[:], b1), (b2_col[:], b2), (b3_col[:], b3)):
                sp.dma_start(dst, src).then_inc(weights_landed, 16)
            sp.wait_ge(zeros_made, 1)
            n = spare_rows * EDGE_DIM // 128
            sp.dma_start(flat[nodes * EDGE_DIM:].rearrange("(p z) -> p z", z=n), zeros[:, 0:n])\
                .then_inc(table_zeroed, 16)

            def load_four(i, zeros):
                for k in range(4):
                    sp.wait_ge(edges_landed[k], 16 * i)
                    load_edges(4 * i + k, k)
                for n in range(zeros):
                    zero_table(ZERO_PER_FOUR * (i - 1) + n)

            zero_fours = ZERO_PARTS // ZERO_PER_FOUR
            with sp.Fori(1, zero_fours + 1) as i:
                load_four(i, ZERO_PER_FOUR)
            with sp.Fori(zero_fours + 1, chunks // 4) as i:
                load_four(i, 0)
            for k in range(2):
                sp.wait_ge(edges_landed[k], 16 * (chunks // 4))
                load_edges(chunks - 2 + k, k)

            def step(s):
                if not s.in_loop and s.group(3) == 0:
                    sp.wait_ge(flags_done, 1)
                if not s.in_loop and s.group(3) == RING - 2:
                    sp.wait_ge(rows_ready, chunks)
                if s.has(3):
                    if s.has(3 - RING):
                        sp.wait_ge(yT_ready, s.done(3 - RING))
                    sp.dma_start(x_in[:, s.slot(3), :],
                                 xT[bass.ds(s.group(3), 1), :, :].rearrange("g p n -> p (g n)"))\
                        .then_inc(x_landed[s.slot(3)], 16)
                if s.has(4):
                    if s.has(4 - AGG_RING):
                        sp.wait_ge(agg_split, s.done(4 - AGG_RING))
                    if not s.in_loop and s.group(4) == 0:
                        sp.wait_ge(dve_setup, NEEDS_READY)
                    need = sp.value_load(tiles_needed[0:1, bass.ds(s.group(4), 1)], min_val=1, max_val=tiles)
                    sp.wait_ge(tiles_landed, need)
                    sp.dma_start(agg_in[:, s.slot(4, AGG_RING), :, :].rearrange("p j c -> p (j c)"),
                                 table[bass.ds(s.first_node(4), GROUP), :]
                                 .rearrange("(p j) c -> p (j c)", j=NODES_J))\
                        .then_inc(agg_landed[s.slot(4, AGG_RING)], 16)
                if s.has(-LAG):
                    sp.wait_ge(norm_done, s.done(-LAG))
                    sp.dma_start(out[bass.ds(s.first_node(-LAG), GROUP), :]
                                 .rearrange("(p j) c -> p (j c)", j=NODES_J),
                                 out_rows[0:NODES_P, s.slot(-LAG, OUT_RING), :, :].rearrange("p j c -> p (j c)"))\
                        .then_inc(out_stored[s.slot(-LAG, OUT_RING)], 16)

            node_steps(sp, step)
            for r in range(OUT_RING):
                sp.wait_ge(out_stored[r], 16 * (groups // OUT_RING))

        @block.gpsimd
        def _(pool):
            nc.gpsimd.memset(ident[:], 0.0).then_inc(ident_made, 1)
            nc.gpsimd.memset(target_parts.bitcast(F32), 0.0).then_inc(parts_cleared, 1)
            nc.gpsimd.memset(lower[:], 1.0).then_inc(lower_made, 1)
            nc.gpsimd.memset(pick[:], 0.0).then_inc(pick_made, 1)
            pool.wait_ge(ident_made, 1)
            nc.gpsimd.affine_select(out=ident[:], in_=ident[:], compare_op=ALU.not_equal, fill=1.0, base=0,
                                    pattern=[[-1, 128]], channel_multiplier=1).then_inc(ident_made, 1)
            pool.wait_ge(lower_made, 1)
            nc.gpsimd.affine_select(out=lower[:], in_=lower[:], compare_op=ALU.is_ge, fill=0.0, base=0,
                                    pattern=[[-1, EDGE_TILE]], channel_multiplier=1).then_inc(lower_made, 1)
            for n, base in enumerate((0, -LO_ROWS)):
                pool.wait_ge(pick_made, n + 1)
                nc.gpsimd.affine_select(out=pick[:], in_=pick[:], compare_op=ALU.not_equal, fill=1.0, base=base,
                                        pattern=[[-1, chunks + 1]], channel_multiplier=1).then_inc(pick_made, 1)
            nc.gpsimd.memset(zeros[:, 0:zero_cols], 0.0).then_inc(zeros_made, 1)
            nc.gpsimd.memset(below[:], -1.0).then_inc(pool_setup, 1)
            nc.gpsimd.iota(spare[:], [[EDGE_TILE, CHUNK]], base=nodes, channel_multiplier=1,
                           allow_small_or_imprecise_dtypes=True).then_inc(consts_made, 1)
            nc.gpsimd.iota(tile_no[:], [[1, CHUNK]], base=1, channel_multiplier=CHUNK,
                           allow_small_or_imprecise_dtypes=True).then_inc(consts_made, 1)
            nc.gpsimd.iota(group_start[:], [[-GROUP, groups]], base=(groups - 1) * GROUP, channel_multiplier=0,
                           allow_small_or_imprecise_dtypes=True).then_inc(consts_made, 1)

            pool.wait_ge(consts_made, 3)
            pool.wait_ge(dve_setup, RANGES_DONE)
            for u in range(CHUNK):
                nc.gpsimd.tensor_scalar(reach[:, u, :], group_start[:], tile_max[:, u:u + 1], tile_no[:, u:u + 1],
                                        ALU.is_le, ALU.mult).then_inc(reach_made, 1)

            pool.wait_ge(dve_setup, ROWS_DONE)
            for n in range(IN_FLIGHT - 1):
                back = n + 1
                nc.gpsimd.tensor_tensor(below[:, n, back:], min_row[:, back:], max_row[:, :tiles - back],
                                        ALU.subtract).then_inc(pool_setup, 1)
                nc.gpsimd.tensor_tensor(above[:, n, back:], min_row[:, :tiles - back], max_row[:, back:],
                                        ALU.subtract).then_inc(pool_setup, 1)
            pool.wait_ge(pool_setup, 7)
            for n in range(IN_FLIGHT - 1):
                back = n + 1
                nc.gpsimd.tensor_tensor(below[:, n, back:], below[:, n, back:], above[:, n, back:], ALU.mult)\
                    .then_inc(pool_setup, 1)
            pool.wait_ge(pool_setup, 10)
            nc.gpsimd.tensor_scalar(above[:], below[:], 0.0, None, ALU.is_ge).then_inc(pool_setup, 1)
            pool.wait_ge(pool_setup, 11)
            nc.gpsimd.tensor_tensor(below[:, 0, :], above[:, 0, :], above[:, 1, :], ALU.add).then_inc(pool_setup, 1)
            pool.wait_ge(pool_setup, 12)
            nc.gpsimd.tensor_tensor(below[:, 1, :], below[:, 0, :], above[:, 2, :], ALU.add).then_inc(pool_setup, 1)
            pool.wait_ge(pool_setup, 13)
            nc.gpsimd.tensor_copy(conflict[:], below[:, 1, :]).then_inc(flags_done, 1)

            pool.wait_ge(weights_landed, 16 * 8)
            nc.gpsimd.tensor_scalar(w3_raw[:], w3_raw[:], 0.5, None, ALU.mult).then_inc(weights_split, 1)
            nc.gpsimd.tensor_scalar(b3_half[:], b3_col[:], 0.5, None, ALU.mult).then_inc(weights_split, 1)
            pool.wait_ge(weights_split, 2)
            parts = ((w1x_raw, w1x_hi, w1x_lo), (w1e_raw, w1e_hi, w1e_lo), (w2_raw, w2_hi, w2_lo),
                     (w3_raw, w3_hi, w3_lo))
            for raw, hi, lo in parts:
                nc.gpsimd.tensor_copy(hi[:], raw[:]).then_inc(weights_split, 1)
            pool.wait_ge(weights_split, 2 + len(parts))
            for raw, hi, lo in parts:
                nc.gpsimd.tensor_tensor(lo[:], raw[:], hi[:].bitcast(F32), ALU.subtract).then_inc(weights_split, 1)

            pool.wait_ge(flags_done, 1)
            pool.wait_ge(table_zeroed, 16 * zero_dmas)

            def landed(c, u, back):
                v = u - back
                pool.wait_ge(scattered[v % CHUNK], 16 * (c + v // CHUNK + 1))

            def scatter_chunk(c, b, first=False):
                pool.wait_ge(sums_stored, c + 1)
                nc.gpsimd.tensor_copy(sums_out[:, b, :, :].rearrange("p u c -> p (u c)"),
                                      edges[:, bass.ds(c * CHUNK, CHUNK), :].rearrange("p u c -> p (u c)"))\
                    .then_inc(copied_out, 1)
                pool.wait_ge(rows_ready, c + 1)
                nc.gpsimd.tensor_copy(rows_out[:, b, :], scatter_rows[:, bass.ds(c * CHUNK, CHUNK)])\
                    .then_inc(copied_out, 1)
                pool.wait_ge(copied_out, 2 * c + 2)
                for u in range(CHUNK):
                    if not first or u >= IN_FLIGHT:
                        landed(c, u, IN_FLIGHT)
                        pool.sem_inc(tiles_landed, 1)
                    if not first or u > 0:
                        flag = pool.value_load(conflict[0:1, bass.ds(c * CHUNK + u, 1)], min_val=0, max_val=IN_FLIGHT - 1)
                        with pool.If(flag > 0):
                            for back in range(1, IN_FLIGHT):
                                if not first or u >= back:
                                    landed(c, u, back)
                    nc.gpsimd.indirect_dma_start(
                        table, bass.IndirectOffsetOnAxis(ap=rows_out[:, b, u:u + 1], axis=0),
                        sums_out[:, b, u, :], None, bounds_check=nodes + spare_rows - 1, oob_is_err=True,
                        compute_op=ALU.add).then_inc(scattered[u], 16)

            scatter_chunk(0, 0, first=True)
            scatter_chunk(1, 1)
            with pool.Fori(1, chunks // 2) as i:
                for b in range(2):
                    scatter_chunk(2 * i + b, b)
            for u in range(IN_FLIGHT):
                landed(chunks, u, IN_FLIGHT)
                pool.sem_inc(tiles_landed, 1)

        @block.tensor
        def _(pe):
            pe.wait_ge(ident_made, 2)

            for k in range(WARM_UP):
                nc.tensor.matmul(t_row_ps[k % 4][:, 0:128], ident[:], ident[:], start=True, stop=True)

            def spread_targets(c, b, times=3):
                pe.wait_ge(selected, c + 1)
                for n in range(2):
                    if not isinstance(c, int) or c > 1:
                        pe.wait_ge(t_row_ready, 2 * c + n - 3)
                    half = slice(n * (CHUNK // 2) * EDGE_TILE, (n + 1) * (CHUNK // 2) * EDGE_TILE)
                    for _ in range(times if n == 0 else 1):
                        last = nc.tensor.matmul(t_row_ps[2 * b + n][0:EDGE_TILE, 0:CHUNK // 2 * EDGE_TILE],
                                                select[:, b, :], target_parts[:, half], start=True, stop=True)
                    last.then_inc(spread, 1)

            def keep_awake(times):
                for _ in range(times):
                    nc.tensor.matmul(bank[6][0:EDGE_TILE, 0:CHUNK // 2 * EDGE_TILE], select[:, 0, :],
                                     target_parts[:, 0:CHUNK // 2 * EDGE_TILE], start=True, stop=True)

            def sum_chunk(c, b, k=None):
                if isinstance(c, int):
                    pe.wait_ge(edges_landed[c % 4], 16 * (c // 4 + 1))
                else:
                    pe.wait_ge(edges_landed[k], 4 * (c - k) + 16)
                if not isinstance(c, int) or c > 1:
                    pe.wait_ge(sums_stored, c - 1)
                for u in range(CHUNK):
                    if u % 2 == 0:
                        pe.wait_ge(matched, c * CHUNK + u + 2)
                    last = nc.tensor.matmul(sums_ps[b][0:EDGE_TILE, u * EDGE_DIM:(u + 1) * EDGE_DIM],
                                            match[b][:, u, :],
                                            edges[:, bass.ds(c * CHUNK, CHUNK), :][:, u, :],
                                            start=True, stop=True)
                last.then_inc(summed, 1)

            pe.wait_ge(parts_ready, 1)
            spread_targets(0, 0)
            spread_targets(1, 1)
            spread_targets(2, 0)
            sum_chunk(0, 0)
            spread_targets(3, 1)
            sum_chunk(1, 1)
            for c in range(2, 2 + PART_CHUNKS):
                spread_targets(c + 2, c % 2, times=4)
                sum_chunk(c, c % 2)
                if c == RANGES_CHUNK:
                    pe.wait_ge(dve_setup, RANGES_DONE)
                    for u in range(CHUNK):
                        nc.tensor.matmul(bank[6][0:1, u * chunks:(u + 1) * chunks], tile_min[:, u:u + 1],
                                         ident[0:chunks, 0:chunks], start=True, stop=True)
                        last = nc.tensor.matmul(bank[7][0:1, u * chunks:(u + 1) * chunks], tile_max[:, u:u + 1],
                                                ident[0:chunks, 0:chunks], start=True, stop=True)
                    last.then_inc(ranges_rowed, 1)
                if c == REACH_CHUNK:
                    pe.wait_ge(dve_setup, REACH_DONE)
                    for h in range(2):
                        last = nc.tensor.matmul(bank[6 + h][0:g_half, 0:chunks],
                                                reach_max[:, h * g_half:(h + 1) * g_half],
                                                ident[0:chunks, 0:chunks], start=True, stop=True)
                    last.then_inc(reach_rowed, 1)
                if c == NEED_CHUNK:
                    pe.wait_ge(dve_setup, NEED_DONE)
                    for h in range(2):
                        last = nc.tensor.matmul(bank[6][0:1, h * g_half:(h + 1) * g_half], need_col[:, h:h + 1],
                                                ident[0:g_half, 0:g_half], start=True, stop=True)
                    last.then_inc(need_rowed, 1)
            with pe.Fori((2 + PART_CHUNKS) // 4, chunks // 4) as i:
                for k in range(4):
                    spread_targets(4 * i + k + 2, k % 2)
                    sum_chunk(4 * i + k, k % 2, k)
            pe.wait_ge(dve_setup, NEEDS_READY)
            keep_awake(3)
            sum_chunk(chunks - 2, 0)
            keep_awake(3)
            sum_chunk(chunks - 1, 1)
            keep_awake(5)

            pe.wait_ge(weights_split, 10)
            pe.wait_ge(sums_stored, chunks)
            pe.wait_ge(dve_setup, SETUP_DONE)

            def step(s):
                if s.has(0):
                    d = s.off % 2
                    pe.wait_ge(x_lo_ready, s.done(0))
                    pe.wait_ge(aggT_ready, s.done(0))
                    for m in range(HALVES):
                        cols = slice(m * 128, (m + 1) * 128)
                        if s.has(-1):
                            pe.wait_ge(h1_ready, s.done(-1, per=2, plus=m + 1))
                        o = l1_ps[m][:, 0:GROUP]
                        nc.tensor.matmul(o, w1x_hi[:, cols], x_hi[:, d, :], start=True, stop=False)
                        nc.tensor.matmul(o, w1x_hi[:, cols], x_lo[:, d, :], start=False, stop=False)
                        nc.tensor.matmul(o, w1x_lo[:, cols], x_hi[:, d, :], start=False, stop=False)
                        nc.tensor.matmul(o, w1e_hi[:, cols], aggT[:, d, :], start=False, stop=False)
                        nc.tensor.matmul(o, w1e_lo[:, cols], aggT[:, d, :], start=False, stop=True)\
                            .then_inc(l1_done, 1)
                if s.has(1):
                    d = (s.off + 1) % 2
                    pe.wait_ge(agg_split, s.done(1))
                    if s.has(0):
                        pe.wait_ge(aggT_ready, s.done(0))
                    for j in range(NODES_J):
                        last = nc.tensor.matmul(
                            aggT_ps[0:2 * EDGE_DIM, j * TURNED:(j + 1) * TURNED],
                            agg_hl[:, d, j, :, :].rearrange("p h c -> p (h c)"),
                            ident_r[:], start=True, stop=True)
                    last.then_inc(aggT_done, 1)
                if s.has(-2):
                    d = s.off % 2
                    o = l3_ps[:, 0:GROUP]
                    if s.has(-3):
                        pe.wait_ge(yT_ready, s.done(-3))
                    for t in range(HALVES):
                        pe.wait_ge(h2_lo_ready, s.done(-2, per=2, plus=t + 1))
                        nc.tensor.matmul(o, w3_hi[:, t, :], h2_hi[:, d, t, :], start=(t == 0), stop=False)
                        nc.tensor.matmul(o, w3_hi[:, t, :], h2_lo[:, d, t, :], start=False, stop=False)
                        last = nc.tensor.matmul(o, w3_lo[:, t, :], h2_hi[:, d, t, :], start=False,
                                                stop=(t == HALVES - 1))
                    last.then_inc(l3_done, 1)
                if s.has(-1):
                    d = (s.off - 1) % 2
                    pe.wait_ge(h1_lo_ready, s.done(-1))
                    for m in range(HALVES):
                        cols = slice(m * 128, (m + 1) * 128)
                        if s.has(-2):
                            pe.wait_ge(h2_ready, s.done(-2, per=2, plus=m + 1))
                        o = l2_ps[m][:, 0:GROUP]
                        for t in range(HALVES):
                            nc.tensor.matmul(o, w2_hi[:, t, cols], h1_hi[:, d, t, :], start=(t == 0), stop=False)
                            nc.tensor.matmul(o, w2_hi[:, t, cols], h1_lo[:, d, t, :], start=False, stop=False)
                            last = nc.tensor.matmul(o, w2_lo[:, t, cols], h1_hi[:, d, t, :], start=False,
                                                    stop=(t == HALVES - 1))
                        last.then_inc(l2_done, 1)
                if s.has(-3):
                    d = (s.off - 3) % 2
                    pe.wait_ge(yT_ready, s.done(-3))
                    if s.has(-4):
                        pe.wait_ge(y_rows_ready, s.done(-4))
                    for j in range(NODES_J):
                        last = nc.tensor.transpose(yT_ps[0:NODES_P, j * NODE_DIM:(j + 1) * NODE_DIM],
                                                   yT[:, d, j * NODES_P:(j + 1) * NODES_P], ident[:])
                    last.then_inc(y_turned, 1)

            node_steps(pe, step)

        @block.scalar
        def _(act):
            def copy_targets(c, b):
                for n in range(2):
                    act.wait_ge(spread, 2 * c + n + 1)
                    if not isinstance(c, int) or c > 1:
                        act.wait_ge(matched, (c - 2) * CHUNK + 4 * n + 4)
                    nc.scalar.activation(
                        t_row[:, b, 4 * n:4 * n + 4, :].rearrange("p u e -> p (u e)"),
                        t_row_ps[2 * b + n][0:EDGE_TILE, 0:4 * EDGE_TILE], ACT.Copy).then_inc(t_row_ready, 1)

            def store_sums(c, b):
                act.wait_ge(summed, c + 1)
                nc.scalar.activation(
                    edges[:, bass.ds(c * CHUNK, CHUNK), :].rearrange("p u c -> p (u c)"),
                    sums_ps[b][0:EDGE_TILE, 0:CHUNK * EDGE_DIM], ACT.Copy).then_inc(sums_stored, 1)

            act.wait_ge(ident_made, 2)
            nc.scalar.activation(silu_probe[:], ident[:, 0:1], ACT.Silu).then_inc(silu_loaded, 1)

            copy_targets(0, 0)
            copy_targets(1, 1)
            copy_targets(2, 0)
            store_sums(0, 0)
            copy_targets(3, 1)
            store_sums(1, 1)
            for c in (2, 3):
                copy_targets(c + 2, c % 2)
                store_sums(c, c % 2)
            with act.Fori(1, chunks // 4) as i:
                for k in range(4):
                    copy_targets(4 * i + k + 2, k % 2)
                    store_sums(4 * i + k, k % 2)
            store_sums(chunks - 2, 0)
            store_sums(chunks - 1, 1)

            act.wait_ge(weights_landed, 16 * 8)

            def step(s):
                if s.has(1):
                    d = (s.off + 1) % 2
                    act.wait_ge(x_landed[s.slot(1)], s.landed(1))
                    if s.has(-1):
                        act.wait_ge(l1_done, s.done(-1, per=2))
                    nc.scalar.activation(x_hi[:, d, :], x_in[:, s.slot(1), :], ACT.Copy).then_inc(x_hi_ready, 1)
                if s.has(0):
                    d = s.off % 2
                    if s.has(-1):
                        act.wait_ge(h1_lo_ready, s.done(-1))
                    for m in range(HALVES):
                        act.wait_ge(l1_done, s.done(0, per=2, plus=m + 1))
                        nc.scalar.activation(h1[:, m, :], l1_ps[m][:, 0:GROUP], ACT.Silu,
                                             bias=b1_col[:, m:m + 1]).then_inc(h1_ready, 1)
                if s.has(1):
                    d = (s.off + 1) % 2
                    act.wait_ge(aggT_done, s.done(1))
                    nc.scalar.activation(
                        aggT[:, d, :].rearrange("p (j q) -> p j q", j=NODES_J),
                        aggT_ps[0:2 * EDGE_DIM, 0:NODES_J * TURNED].rearrange("p (j q) -> p j q", j=NODES_J)
                        [:, :, 0:NODES_P], ACT.Copy)\
                        .then_inc(aggT_ready, 1)
                if s.has(0):
                    d = s.off % 2
                    act.wait_ge(h1_ready, s.done(0, per=2))
                    if s.has(-2):
                        act.wait_ge(l2_done, s.done(-2, per=2))
                    nc.scalar.activation(h1_hi[:, d, :, :].rearrange("p t n -> p (t n)"),
                                         h1[:].rearrange("p t n -> p (t n)"), ACT.Copy)\
                        .then_inc(h1_hi_ready, 1)
                if s.has(-1):
                    d = (s.off - 1) % 2
                    if s.has(-2):
                        act.wait_ge(h2_lo_ready, s.done(-2, per=2))
                    for m in range(HALVES):
                        act.wait_ge(l2_done, s.done(-1, per=2, plus=m + 1))
                        nc.scalar.activation(h2[:, m, :], l2_ps[m][:, 0:GROUP], ACT.Silu,
                                             bias=b2_col[:, m:m + 1]).then_inc(h2_ready, 1)
                        act.wait_ge(h2_ready, s.done(-1, per=2, plus=m + 1))
                        if s.has(-3):
                            act.wait_ge(l3_done, s.done(-3))
                        nc.scalar.activation(h2_hi[:, d, m, :], h2[:, m, :], ACT.Copy).then_inc(h2_hi_ready, 1)
                if s.has(-3):
                    act.wait_ge(y_turned, s.done(-3))
                    if s.has(-3 - RING):
                        act.wait_ge(norm_done, s.done(-3 - RING))
                    nc.scalar.activation(y_rows[:, s.slot(-3), :, :].rearrange("p j c -> p (j c)"),
                                         yT_ps[0:NODES_P, :], ACT.Copy).then_inc(y_rows_ready, 1)

            node_steps(act, step)

        @block.vector
        def _(dve):
            dve.wait_ge(by_chunk_landed, 32)
            top, bottom = slice(0, chunks), slice(LO_ROWS, LO_ROWS + chunks)
            raw = targets_by_chunk.rearrange("p u e -> p (u e)")
            nc.vector.tensor_copy(targets_hi[bottom, :], raw[bottom, :]).then_inc(dve_setup, 1)
            dve.wait_ge(dve_setup, 1)
            dve.wait_ge(parts_cleared, 1)
            nc.vector.tensor_copy(target_parts[top, :], raw[top, :])
            nc.vector.tensor_tensor(target_parts[bottom, :], raw[bottom, :], targets_hi[bottom, :].bitcast(F32),
                                    ALU.subtract).then_inc(parts_ready, 1)
            def select_chunk(c, b):
                if not isinstance(c, int) or c > 1:
                    dve.wait_ge(spread, 2 * c - 2)
                nc.vector.tensor_copy(select[:, b, :], pick[:, bass.ds(c, 1)].to_broadcast([128, EDGE_TILE]))\
                    .then_inc(selected, 1)

            dve.wait_ge(pick_made, 3)
            select_chunk(0, 0)
            select_chunk(1, 1)
            dve.wait_ge(targets_landed, 16)
            nc.vector.tensor_copy(t_col, targets[:]).then_inc(cols_ready, 1)
            dve.wait_ge(cols_ready, 1)

            def choose_spare(c, b):
                dve.wait_ge(matched, (c + 1) * CHUNK)
                if not isinstance(c, int) or c > 1:
                    dve.wait_ge(rows_ready, c - 1)
                nc.vector.scalar_tensor_tensor(go_spare[:, b, :], n_match[:, b, :], 1.5,
                                               to_spare[:, bass.ds(c * CHUNK, CHUNK)],
                                               ALU.is_gt, ALU.mult).then_inc(spare_chosen, 1)

            def choose_rows(c, b):
                dve.wait_ge(spare_chosen, c + 1)
                nc.vector.tensor_tensor(scatter_rows[:, bass.ds(c * CHUNK, CHUNK)], go_spare[:, b, :],
                                        targets[:, bass.ds(c * CHUNK, CHUNK)], ALU.add).then_inc(rows_ready, 1)

            def match_chunk(c, b, more=True, parts=()):
                first = isinstance(c, int) and c == 0
                if not isinstance(c, int) or c > 1:
                    dve.wait_ge(summed, c - 1)
                    dve.wait_ge(spare_chosen, c - 1)
                for u in range(CHUNK):
                    if u % 4 == 0:
                        dve.wait_ge(t_row_ready, 2 * c + u // 4 + 1)
                    nc.vector.scalar_tensor_tensor(match[b][:, u, :], t_row[:, b, u, :],
                                                   t_col[:, bass.ds(c * CHUNK, CHUNK)][:, u:u + 1], lower[:], ALU.is_equal,
                                                   ALU.mult, accum_out=n_match[:, b, u:u + 1]).then_inc(matched, 1)
                    if first and u == 0:
                        select_chunk(2, 0)
                    if u == 3 and more:
                        select_chunk(c + 3, 1 - b)
                    if u == 2 and not first:
                        choose_spare(c - 1, 1 - b)
                    if u == 4 and not first:
                        choose_rows(c - 1, 1 - b)
                    if u % 2 == 1 and u // 2 < len(parts):
                        setup_part(parts[u // 2])

            assert (2 + PART_CHUNKS) % 4 == 0 and chunks >= PART_CHUNKS + 8

            def setup_part(k):
                if k < 4:
                    half = slice(k % 2 * (CHUNK // 2), (k % 2 + 1) * (CHUNK // 2))
                    to, op = ((tile_min, ALU.min), (tile_max, ALU.max))[k // 2]
                    ins = nc.vector.tensor_reduce(to[:, half], targets_by_chunk[0:chunks, half, :], AX_X, op)
                elif k < 6:
                    row, ps = ((min_row, bank[6]), (max_row, bank[7]))[k - 4]
                    dve.wait_ge(ranges_rowed, 1)
                    ins = nc.vector.tensor_copy(row.rearrange("o (c u) -> o c u", u=CHUNK),
                                                ps[0:1, 0:tiles].rearrange("o (u c) -> o c u", u=CHUNK))
                elif k < 10:
                    dve.wait_ge(reach_made, CHUNK)
                    n = groups // 4
                    part = slice((k - 6) * n, (k - 5) * n)
                    ins = nc.vector.tensor_reduce(reach_max[:, part], reach[:, :, part].rearrange("p u g -> p g u"),
                                                  AX_X, ALU.max)
                elif k < 12:
                    h = k - 10
                    dve.wait_ge(reach_rowed, 1)
                    ins = nc.vector.tensor_reduce(need_col[:, h:h + 1], bank[6 + h][0:g_half, 0:chunks], AX_X, ALU.max)
                elif k == 12:
                    dve.wait_ge(need_rowed, 1)
                    ins = nc.vector.tensor_scalar(tiles_needed[:], bank[6][0:1, 0:groups], 1.0, None, ALU.max)
                else:
                    ins = nc.vector.tensor_copy(ident_r[:], ident[0:NODES_P, 0:TURNED])
                ins.then_inc(dve_setup, 1)

            match_chunk(0, 0)
            dve.wait_ge(consts_made, 1)
            nc.vector.tensor_tensor(to_spare.rearrange("p (c u) -> p c u", u=CHUNK),
                                    spare[:].rearrange("p (o u) -> p o u", o=1).to_broadcast([EDGE_TILE, chunks, CHUNK]),
                                    t_col.rearrange("p (c u) -> p c u", u=CHUNK), ALU.subtract).then_inc(cols_ready, 1)
            dve.wait_ge(cols_ready, 2)
            match_chunk(1, 1)
            dve.wait_ge(consts_made, 3)
            for c in range(2, 2 + PART_CHUNKS):
                match_chunk(c, c % 2, parts=CHUNK_PARTS[c])
            with dve.Fori((2 + PART_CHUNKS) // 4, chunks // 4) as i:
                for k in range(4):
                    match_chunk(4 * i + k, k % 2)
            match_chunk(chunks - 2, 0, more=False)
            match_chunk(chunks - 1, 1, more=False)
            choose_spare(chunks - 1, 1)
            choose_rows(chunks - 1, 1)
            dve.wait_ge(weights_split, 10)

            NORM_OPS = 18
            tt, stt, ts = nc.vector.tensor_tensor, nc.vector.scalar_tensor_tensor, nc.vector.tensor_scalar
            tmp = [st[:, k, :] for k in range(8)]

            def norm_op(s, lag, k):
                first = s.slot(-lag)
                q = first // NORM_BATCH
                view = stats[:, first:first + NORM_BATCH, :, :].rearrange("p g j f -> p (g j) f")
                before = (s.ring_no * (RING // NORM_BATCH) + (s.off - lag) // NORM_BATCH) * NORM_OPS
                if k not in (0, 1, 2, 4):
                    dve.wait_ge(norm_chain, before + k)
                if k == 0:
                    ins = tt(tmp[0], view[:, :, 1], view[:, :, 4], ALU.add)
                elif k == 1:
                    ins = tt(tmp[1], view[:, :, 1], view[:, :, 4], ALU.subtract)
                elif k == 2:
                    ins = tt(tmp[2], view[:, :, 2], view[:, :, 5], ALU.add)
                elif k == 3:
                    ins = tt(tmp[3], tmp[1], tmp[1], ALU.mult)
                elif k == 4:
                    dve.wait_ge(norm_chain, before + 1)
                    ins = ts(mean[:, q, :], tmp[0], 0.5, None, ALU.mult)
                elif k == 5:
                    ins = stt(tmp[4], tmp[3], NODE_DIM / 4.0, tmp[2], ALU.mult, ALU.add)
                elif k == 6:
                    ins = ts(tmp[5], tmp[4], 1.0 / NODE_DIM, EPS / 4.0, ALU.mult, ALU.add)
                elif k == 7:
                    ins = ts(tmp[6].bitcast(I32), tmp[5].bitcast(I32), 1, None, ALU.logical_shift_right)
                elif k == 8:
                    ins = ts(tmp[7].bitcast(I32), tmp[6].bitcast(I32), -1.0, float(0x5F3759DF), ALU.mult, ALU.add)
                else:
                    turn, part = divmod(k - 9, 3)
                    y, other = (tmp[7], tmp[6]) if turn % 2 == 0 else (tmp[6], tmp[7])
                    if part == 0:
                        ins = tt(tmp[3], y, y, ALU.mult)
                    elif part == 1:
                        ins = stt(tmp[4], tmp[3], -0.5, tmp[5], ALU.mult, ALU.mult)
                    else:
                        ins = stt(rstd[:, q, :] if turn == 2 else other, tmp[4], 1.5, y, ALU.add, ALU.mult)
                ins.then_inc(norm_chain, 1)

            def step(s):
                first_half = s.off % NORM_BATCH == NORM_BATCH - 1 and s.has(-4)
                second_half = s.off % NORM_BATCH == 0 and s.has(-5)

                def norm_part(k1, k2):
                    if first_half and k1 is not None:
                        norm_op(s, 7, k1)
                    if second_half and k2 is not None:
                        norm_op(s, 8, 9 + k2)

                if s.has(-4):
                    dve.wait_ge(y_rows_ready, s.done(-4))
                    for j in range(NODES_J):
                        last = nc.vector.bn_stats(stats[:, s.slot(-4), j, :], y_rows[:, s.slot(-4), j, :])
                        norm_part(None, j)
                    last.then_inc(stats_ready, 1)
                elif second_half:
                    for k in range(NODES_J):
                        norm_part(None, k)
                if s.has(2):
                    d = s.off % 2
                    dve.wait_ge(agg_landed[s.slot(2, AGG_RING)], s.landed(2, AGG_RING))
                    if s.has(0):
                        dve.wait_ge(aggT_done, s.done(0))
                    nc.vector.tensor_copy(agg_hl[:, d, :, 0, :], agg_in[:, s.slot(2, AGG_RING), :, :])\
                        .then_inc(agg_hi_ready, 1)
                if first_half:
                    dve.wait_ge(stats_ready, s.done(-4))
                norm_part(0, None)
                if s.has(-LAG):
                    q = s.slot(-LAG) // NORM_BATCH
                    if s.has(-LAG - OUT_RING):
                        dve.wait_ge(out_stored[s.slot(-LAG, OUT_RING)], s.landed(-LAG - OUT_RING, OUT_RING))
                    if s.slot(-LAG, NORM_BATCH) == 0:
                        dve.wait_ge(norm_chain, (s.ring_no * (RING // NORM_BATCH) + (s.off - LAG) // NORM_BATCH + 1)
                                    * NORM_OPS)
                    for j in range(NODES_J):
                        k = s.slot(-LAG, NORM_BATCH) * NODES_J + j
                        last = nc.vector.tensor_scalar(out_rows[0:NODES_P, s.slot(-LAG, OUT_RING), j, :],
                                                       y_rows[:, s.slot(-LAG), j, :],
                                                       mean[:, q, k:k + 1], rstd[:, q, k:k + 1],
                                                       ALU.subtract, ALU.mult)
                        if j < NODES_J - 1:
                            norm_part(1 + j, 4 + j)
                    last.then_inc(norm_done, 1)
                else:
                    for k in range(NODES_J - 1):
                        norm_part(1 + k, 4 + k)
                norm_part(4, 7)
                if s.has(2):
                    dve.wait_ge(agg_hi_ready, s.done(2))
                    nc.vector.tensor_tensor(agg_hl[:, d, :, 1, :], agg_in[:, s.slot(2, AGG_RING), :, :],
                                            agg_hl[:, d, :, 0, :].bitcast(F32), ALU.subtract).then_inc(agg_split, 1)
                norm_part(5, 8)
                if s.has(1):
                    d = (s.off + 1) % 2
                    dve.wait_ge(x_hi_ready, s.done(1))
                    nc.vector.tensor_tensor(x_lo[:, d, :], x_in[:, s.slot(1), :], x_hi[:, d, :].bitcast(F32),
                                            ALU.subtract).then_inc(x_lo_ready, 1)
                norm_part(6, None)
                if s.has(0):
                    d = s.off % 2
                    dve.wait_ge(h1_hi_ready, s.done(0))
                    nc.vector.tensor_tensor(h1_lo[:, d, :, :].rearrange("p t n -> p (t n)"),
                                            h1[:].rearrange("p t n -> p (t n)"),
                                            h1_hi[:, d, :, :].rearrange("p t n -> p (t n)").bitcast(F32),
                                            ALU.subtract).then_inc(h1_lo_ready, 1)
                norm_part(7, None)
                if s.has(-2):
                    d = s.off % 2
                    dve.wait_ge(l3_done, s.done(-2))
                    if s.has(-4):
                        dve.wait_ge(y_turned, s.done(-4))
                    nc.vector.scalar_tensor_tensor(yT[:, d, :], l3_ps[:, 0:GROUP], b3_half[:],
                                                   x_in[:, s.slot(-2), :], ALU.add, ALU.add)\
                        .then_inc(yT_ready, 1)
                norm_part(8, None)
                if s.has(-1):
                    d = (s.off - 1) % 2
                    if s.has(-3):
                        dve.wait_ge(l3_done, s.done(-3))
                    for m in range(HALVES):
                        dve.wait_ge(h2_hi_ready, s.done(-1, per=2, plus=m + 1))
                        nc.vector.tensor_tensor(h2_lo[:, d, m, :], h2[:, m, :], h2_hi[:, d, m, :].bitcast(F32),
                                                ALU.subtract).then_inc(h2_lo_ready, 1)

            node_steps(dve, step)


def kernel(x, src, dst, edge_attr_48, L0_gnn_W1, L0_gnn_b1, L0_gnn_W2, L0_gnn_b2, L0_gnn_W3, L0_gnn_b3):
    import concourse.bacc as bacc
    from concourse.bass_utils import run_bass_kernel_spmd

    x = np.asarray(x)
    nodes = x.shape[0]
    groups = nodes // GROUP
    tiles = np.shape(dst)[0] // EDGE_TILE
    assert tiles % ORDER_BLOCK == 0
    order = np.array([tiles - 1 - (k // ORDER_BLOCK * ORDER_BLOCK + k * TILE_STRIDE % ORDER_BLOCK) for k in range(tiles)])
    by_tile = np.asarray(dst).reshape(tiles, EDGE_TILE)[order]
    arrays = {
        "xT": x.reshape(groups, NODES_P, NODES_J, NODE_DIM)[::-1].transpose(0, 3, 2, 1)
        .reshape(groups, NODE_DIM, GROUP),
        "edge_rows": np.asarray(edge_attr_48).reshape(tiles, EDGE_TILE, EDGE_DIM)[order].transpose(1, 0, 2),
        "target_cols": by_tile.T,
        "target_rows": by_tile.reshape(tiles // CHUNK, CHUNK, EDGE_TILE),
        "W1": np.asarray(L0_gnn_W1),
        "b1": np.asarray(L0_gnn_b1).reshape(HALVES, 128).T,
        "W2": np.asarray(L0_gnn_W2),
        "b2": np.asarray(L0_gnn_b2).reshape(HALVES, 128).T,
        "W3": np.asarray(L0_gnn_W3),
        "b3": np.asarray(L0_gnn_b3).reshape(NODE_DIM, 1),
    }
    arrays = {name: np.ascontiguousarray(a) for name, a in arrays.items()}
    nc = bacc.Bacc("TRN2", target_bir_lowering=False, num_devices=1)
    args = [nc.dram_tensor(name, a.shape, mybir.dt.from_np(a.dtype), kind="ExternalInput").ap()
            for name, a in arrays.items()]
    out = nc.dram_tensor("out", (nodes, NODE_DIM), F32, kind="ExternalOutput").ap()
    build_gnn(nc, *args, out)
    r = run_bass_kernel_spmd(nc, [arrays], core_ids=[0])
    return r.results[0]["out"]
```
